# Optimizing a Trainium2 kernel written in Bass

```python
import numpy as np
import jax
import jax.numpy as jnp

def _softmax(x, axis=-1):
    return jax.nn.softmax(x, axis=axis)

def _gelu(x):
    return jax.nn.gelu(x, approximate=True)

def _silu(x):
    return jax.nn.silu(x)

def _sigmoid(x):
    return jax.nn.sigmoid(x)

def _layernorm(x, axis=-1, eps=1e-05):
    m = jnp.mean(x, axis=axis, keepdims=True)
    v = jnp.var(x, axis=axis, keepdims=True)
    return (x - m) / jnp.sqrt(v + eps)

def _scatter_add(tgt, idx, src, axis=0):
    return tgt.at[idx].add(src)

def _segment_sum(src, seg, n):
    return jax.ops.segment_sum(src, seg, n)
kernel_name = 'mk_adj_ffn_d1_adj_r2_c386f8'

def setup_inputs(seed: int=0):
    np.random.seed(seed)
    _w = jnp.asarray

    def _rec_inputs():
        import jax
        import jax.numpy as jnp
        _gk = jax.random.key(seed)
        x = -0.0002928 + 1 * jax.random.normal(jax.random.fold_in(_gk, 1), (64, 128, 128), jnp.float32)
        _a = jax.random.bernoulli(jax.random.fold_in(_gk, 2), 0.015625, (64, 128, 128))
        _a = jnp.logical_or(_a, jnp.swapaxes(_a, -1, -2))
        _a = jnp.logical_or(_a, jnp.eye(128, dtype=bool))
        adj = _a.astype(jnp.int32)
        return (x, adj)
    x, adj = _rec_inputs()

    def _L0_gnn_setup():
        import jax, jax.numpy as jnp
        import numpy as np
        OUT = 128
        NUM_LAYERS = 3

        def _gru_cell(inp, h, w_ih, w_hh, b_ih, b_hh):
            gi = inp @ w_ih.T + b_ih
            gh = h @ w_hh.T + b_hh
            i_r, i_z, i_n = jnp.split(gi, 3, axis=-1)
            h_r, h_z, h_n = jnp.split(gh, 3, axis=-1)
            r = jax.nn.sigmoid(i_r + h_r)
            z = jax.nn.sigmoid(i_z + h_z)
            n = jnp.tanh(i_n + r * h_n)
            return (1.0 - z) * n + z * h
        key = jax.random.key(seed)
        ks = jax.random.split(key, 8)
        B, N, D = (32, 256, 128)
        x = jax.random.normal(ks[0], (B, N, D), dtype=jnp.float32)
        adj = jax.random.randint(ks[1], (B, N, N), 0, 2, dtype=jnp.int32)
        s = 1.0 / np.sqrt(OUT)
        weight = jax.random.uniform(ks[2], (NUM_LAYERS, OUT, OUT), jnp.float32, -s, s)
        w_ih = jax.random.uniform(ks[3], (3 * OUT, OUT), jnp.float32, -s, s)
        w_hh = jax.random.uniform(ks[4], (3 * OUT, OUT), jnp.float32, -s, s)
        b_ih = jax.random.uniform(ks[5], (3 * OUT,), jnp.float32, -s, s)
        b_hh = jax.random.uniform(ks[6], (3 * OUT,), jnp.float32, -s, s)
        return {'x': x, 'adj': adj, 'weight': weight, 'w_ih': w_ih, 'w_hh': w_hh, 'b_ih': b_ih, 'b_hh': b_hh}
    _L0_gnn_all = _L0_gnn_setup()
    _L0_gnn_in = {k: v for k, v in _L0_gnn_all.items() if k in ('weight', 'w_ih', 'w_hh', 'b_ih', 'b_hh')}
    del _L0_gnn_all

    def _L0_ffn_setup():
        import jax, jax.numpy as jnp
        import numpy as np
        C = 128
        HID = 512
        E = 8
        TEMP = 1.0
        key = jax.random.key(seed)
        ks = jax.random.split(key, 7)
        x = jax.random.normal(ks[0], (8, 8192, C), dtype=jnp.float32)
        W1 = jax.random.normal(ks[1], (C, HID), dtype=jnp.float32) * 0.02
        b1 = jnp.zeros((HID,), dtype=jnp.float32)
        Wg = jax.random.normal(ks[2], (HID, E), dtype=jnp.float32) * 0.02
        bg = jnp.zeros((E,), dtype=jnp.float32)
        Wd = jax.random.normal(ks[3], (E, HID, C), dtype=jnp.float32) * 0.02
        bd = jnp.zeros((E, C), dtype=jnp.float32)
        return {'x': x, 'W1': W1, 'b1': b1, 'Wg': Wg, 'bg': bg, 'Wd': Wd, 'bd': bd}
    _L0_ffn_all = _L0_ffn_setup()
    _L0_ffn_in = {k: v for k, v in _L0_ffn_all.items() if k in ('W1', 'b1', 'Wg', 'bg', 'Wd', 'bd')}
    del _L0_ffn_all
    return {'x': x, 'adj': adj, 'L0_gnn_weight': _L0_gnn_in['weight'], 'L0_gnn_w_ih': _L0_gnn_in['w_ih'], 'L0_gnn_w_hh': _L0_gnn_in['w_hh'], 'L0_gnn_b_ih': _L0_gnn_in['b_ih'], 'L0_gnn_b_hh': _L0_gnn_in['b_hh'], 'L0_ffn_W1': _L0_ffn_in['W1'], 'L0_ffn_b1': _L0_ffn_in['b1'], 'L0_ffn_Wg': _L0_ffn_in['Wg'], 'L0_ffn_bg': _L0_ffn_in['bg'], 'L0_ffn_Wd': _L0_ffn_in['Wd'], 'L0_ffn_bd': _L0_ffn_in['bd']}

def reference(x, adj, L0_gnn_weight, L0_gnn_w_ih, L0_gnn_w_hh, L0_gnn_b_ih, L0_gnn_b_hh, L0_ffn_W1, L0_ffn_b1, L0_ffn_Wg, L0_ffn_bg, L0_ffn_Wd, L0_ffn_bd):
    import jax
    import jax.numpy as jnp

    def _L0_gnn_ref(x, adj, weight, w_ih, w_hh, b_ih, b_hh):
        import jax, jax.numpy as jnp
        import numpy as np
        OUT = 128
        NUM_LAYERS = 3

        def _gru_cell(inp, h, w_ih, w_hh, b_ih, b_hh):
            gi = inp @ w_ih.T + b_ih
            gh = h @ w_hh.T + b_hh
            i_r, i_z, i_n = jnp.split(gi, 3, axis=-1)
            h_r, h_z, h_n = jnp.split(gh, 3, axis=-1)
            r = jax.nn.sigmoid(i_r + h_r)
            z = jax.nn.sigmoid(i_z + h_z)
            n = jnp.tanh(i_n + r * h_n)
            return (1.0 - z) * n + z * h
        A = (adj != 0).astype(x.dtype)
        h = x
        L = weight.shape[0]
        for i in range(L):
            m = jnp.einsum('bnd,de->bne', h, weight[i])
            aggr = jnp.einsum('bst,bsd->btd', A, m)
            h = _gru_cell(aggr, h, w_ih, w_hh, b_ih, b_hh)
        return h

    def _L0_ffn_ref(x, W1, b1, Wg, bg, Wd, bd):
        import jax, jax.numpy as jnp
        import numpy as np
        C = 128
        HID = 512
        E = 8
        TEMP = 1.0
        orig_shape = x.shape
        xf = x.reshape(-1, orig_shape[-1])
        H = jax.nn.gelu(xf @ W1 + b1, approximate=False)
        probs = jax.nn.softmax((H @ Wg + bg) / TEMP, axis=-1)
        assign = jnp.argmax(probs, axis=-1)
        out = jnp.zeros_like(xf)
        for e in range(Wd.shape[0]):
            y = H @ Wd[e] + bd[e]
            sel = (assign == e)[:, None]
            out = out + jnp.where(sel, probs[:, e:e + 1] * y, 0.0)
        return out.reshape(orig_shape)
    x = x + _L0_gnn_ref(_layernorm(x, axis=-1), adj, L0_gnn_weight, L0_gnn_w_ih, L0_gnn_w_hh, L0_gnn_b_ih, L0_gnn_b_hh)
    x = x + _L0_ffn_ref(_layernorm(x, axis=-1), L0_ffn_W1, L0_ffn_b1, L0_ffn_Wg, L0_ffn_bg, L0_ffn_Wd, L0_ffn_bd)
    return x

_drawn_inputs = setup_inputs


def setup_inputs(seed=0):
    import zlib

    import numpy as np

    out = dict(_drawn_inputs(seed))
    spreads = {'L0_ffn_b1': (0.0, 0.8), 'L0_ffn_bg': (0.0, 0.5), 'L0_ffn_bd': (0.0, 0.681)}
    factors = {'L0_ffn_W1': 5.896, 'L0_ffn_Wg': 5.659, 'L0_ffn_Wd': 7.728}
    for name, (base, spread) in spreads.items():
        noise = np.random.default_rng([zlib.crc32(name.encode()), seed]).standard_normal(out[name].shape)
        drawn = base * np.exp(spread * noise) if base else spread * noise
        out[name] = jnp.asarray(drawn.astype(out[name].dtype))
    for name, factor in factors.items():
        out[name] = (out[name] * factor).astype(out[name].dtype)
    return out
```

```python
import concourse.bass as bass
from concourse import mybir
from contextlib import ExitStack


fp32 = mybir.dt.float32
f32r = mybir.dt.float32r
i32 = mybir.dt.int32
u32 = mybir.dt.uint32
ALU = mybir.AluOpType
ACT = mybir.ActivationFunctionType
AX = mybir.AxisListType

P = 128
GR = 4
NT = GR * P
LAYERS = 3
QUAD = 4
UNITS = QUAD * LAYERS


def build(nc, x, adj, W, w_ih, w_hh, b_ih, b_hh, W1, b1, Wg, bg, Wd, bd, out):
    GRAPHS = x.shape[0]
    GROUPS = GRAPHS // GR
    QUADS = GROUPS // QUAD
    TOK = GRAPHS * P
    HID = W1.shape[1]
    KC = HID // P
    E = Wd.shape[0]
    EPS = 1e-5
    REGION = TOK + P
    ROW = P + 4
    MEAN, RSTD, PROB, TOKEN = P, P + 1, P + 2, P + 3
    SLOTS = -(-((TOK + E * (P - 1)) // P) // GR) * GR
    SGROUPS = SLOTS // GR
    RING = 6
    NOBODY = 1 << 20

    h_out = out.rearrange("a n c -> (a n) c")
    sorted_rows = nc.dram_tensor("sorted_rows", ((E + 1) * REGION, ROW), fp32).ap()

    ctx = ExitStack()
    with ctx:
        def sb(name, shape, dt=fp32):
            return ctx.enter_context(nc.sbuf_tensor(name, shape, dt))

        def sem(name):
            return ctx.enter_context(nc.semaphore(name))

        ident = sb("ident", [P, P])
        before = sb("before", [P, P])
        ones = sb("ones", [P, P])
        wraw = sb("wraw", [P, 9, P])
        wT = sb("wT", [P, 6, P])
        whh_hi, whh_lo = sb("whh_hi", [P, 3 * P], f32r), sb("whh_lo", [P, 3 * P], f32r)
        wf_hi, wf_lo = sb("wf_hi", [P, LAYERS, 3 * P], f32r), sb("wf_lo", [P, LAYERS, 3 * P], f32r)
        w1raw = sb("w1raw", [P, HID])
        w1_hi, w1_lo = sb("w1_hi", [P, HID], f32r), sb("w1_lo", [P, HID], f32r)
        b1c = sb("b1c", [P, KC])
        wg_sb = sb("wg_sb", [P, KC, E])
        wd_sb = sb("wd_sb", [P, E * KC * P])
        bd_bc = sb("bd_bc", [P, E * P])
        bg_bc = sb("bg_bc", [P, GR, E])
        bi, bh = sb("bi", [P, 3]), sb("bh", [P, 3])
        bsum = sb("bsum", [P, 3])
        half = sb("half", [P, GR])
        xres = sb("xres", [P, GRAPHS, P])
        adj_i = sb("adj_i", [P, GRAPHS, P], i32)
        A = sb("A", [P, QUAD, NT], f32r)
        hT = sb("hT", [P, QUAD, NT])
        hT_hi, hT_lo = sb("hT_hi", [P, QUAD, NT], f32r), sb("hT_lo", [P, QUAD, NT], f32r)
        hn_hi, hn_lo = sb("hn_hi", [P, 2, NT], f32r), sb("hn_lo", [P, 2, NT], f32r)
        ag_hi, ag_lo = sb("ag_hi", [P, 2, NT], f32r), sb("ag_lo", [P, 2, NT], f32r)
        r_sb, cand = sb("r_sb", [P, 2, NT]), sb("cand", [P, 2, NT])
        n_sb, diff = sb("n_sb", [P, 2, NT]), sb("diff", [P, 2, NT])
        z_sb = sb("z_sb", [P, QUAD, NT])
        xn = sb("xn", [P, QUAD, NT])
        stats = sb("stats", [P, QUAD, GR, 6])
        mv = sb("mv", [P, QUAD, GR, 2])
        rstd = sb("rstd", [P, QUAD, GR])
        stage = sb("stage", [P, 2, GR, ROW])
        ids = sb("ids", [P, GRAPHS], i32)
        lg, sh, mt, oh = (sb(n, [P, 2, GR, E]) for n in ("lg", "sh", "mt", "oh"))
        th, num, den, ex, rk = (sb(n, [P, 2, GR, E]) for n in ("th", "num", "den", "ex", "rk"))
        mx, mv8, ssum, posf = (sb(n, [P, 2, GR]) for n in ("mx", "mv8", "ssum", "posf"))
        pos = sb("pos", [P, 2, GR], u32)
        rev = sb("rev", [P, GR, E])
        ecap = sb("ecap", [P, E])
        base = sb("base", [P, E])
        iot = sb("iot", [P, GR * E], i32)
        ecap_i = sb("ecap_i", [P, E], i32)
        slot_i = sb("slot_i", [1, SLOTS * E], i32)
        z_flat = z_sb[0:1, :, :].rearrange("p q n -> p (q n)")
        slotf = z_flat[:, 0:SLOTS * E].rearrange("o (j e) -> o j e", e=E)
        le = z_flat[:, SLOTS * E:2 * SLOTS * E].rearrange("o (j e) -> o j e", e=E)
        tri_i = sb("tri_i", [1, E, E], i32)
        tri = sb("tri", [1, E, E])
        nf = sb("nf", [1, E])
        ni = sb("ni", [1, E], i32)
        nblk = sb("nblk", [1, E])
        cumt = sb("cumt", [1, E, E])
        cum = sb("cum", [1, E])
        skip = sb("skip", [1, E])
        rsum = sb("rsum", [1, SLOTS])
        esum = sb("esum", [1, SLOTS])
        row_tab, wd_tab, bd_tab = (sb(n, [1, SLOTS], i32) for n in ("row_tab", "wd_tab", "bd_tab"))
        part_i, part = sb("part_i", [P, 1], i32), sb("part", [P, 1])
        padf = sb("padf", [P, E + 1])
        padi = sb("padi", [P, E + 1], u32)
        padrow = sb("padrow", [P, ROW])
        adj_f = adj_i[:, :, :].rearrange("p g n -> p (g n)").bitcast(fp32)
        HT = adj_f[:, 0:2 * KC * NT].rearrange("p (b k n) -> p b k n", b=2, k=KC)
        rows = adj_f[:, 2 * KC * NT:2 * KC * NT + RING * GR * ROW].rearrange(
            "p (b s r) -> p b s r", b=RING, s=GR)
        yb = r_sb[:, :, :].rearrange("p b (s c) -> p b s c", s=GR)
        yo = cand[:, :, :].rearrange("p b (s c) -> p b s c", s=GR)

        bank = [ctx.enter_context(nc.psum_tensor(f"bank{i}", [P, NT], fp32)) for i in range(8)]
        pR, pZ, pGH, pGI, pAG, pT, pF, pX = bank

        w_in = sem("w_in")
        ffn_in = sem("ffn_in")
        b_in = sem("b_in")
        data_in = sem("data_in")
        passed = sem("passed")
        c_id, c_msk, c_gp, c_dv = sem("c_id"), sem("c_msk"), sem("c_gp"), sem("c_dv")
        wt_ps, wt_sb, wf_ps, whh_done = sem("wt_ps"), sem("wt_sb"), sem("wf_ps"), sem("whh_done")
        whi_done, wlo_done = sem("whi_done"), sem("wlo_done")
        w1_hi_done, w1_lo_done = sem("w1_hi_done"), sem("w1_lo_done")
        hh_ps, r_ps, z_ps, in_ps, ag_ps, t_ps, f_ps = (
            sem(n) for n in ("hh_ps", "r_ps", "z_ps", "in_ps", "ag_ps", "t_ps", "f_ps"))
        aghi_ok, r_ok, z_ok, n_ok, hnhi_ok, hthi_ok, h0_ok, h0hi_ok, x0hi_ok = (
            sem(n) for n in ("aghi_ok", "r_ok", "z_ok", "n_ok", "hnhi_ok", "hthi_ok", "h0_ok", "h0hi_ok", "x0hi_ok"))
        aglo_ok, h_ok, hnlo_ok, h0lo_ok, rhn_ok, cand_ok, x1_ok, adj_ok = (
            sem(n) for n in ("aglo_ok", "h_ok", "hnlo_ok", "h0lo_ok", "rhn_ok", "cand_ok", "x1_ok", "adj_ok"))
        bn_ok, mv_ok, var_ok, rstd_ok, xn_ok = (sem(n) for n in ("bn_ok", "mv_ok", "var_ok", "rstd_ok", "xn_ok"))
        diff_ok, zd_ok, htlo_ok, x0lo_ok = (sem(n) for n in ("diff_ok", "zd_ok", "htlo_ok", "x0lo_ok"))
        g_bn, g_mv, g_var, g_rstd, g_xn, g_t, g_xhi, g_xlo, g_w1, g_h, g_lg = (
            sem("g_" + n) for n in ("bn", "mv", "var", "rstd", "xn", "t", "xhi", "xlo", "w1", "h", "lg"))
        g_dve, g_sh, g_oh, g_th, g_rk, g_prob, g_pos, g_stage, g_out, g_pdve, g_tb2, g_base = (
            sem("g_" + n) for n in ("dve", "sh", "oh", "th", "rk", "prob", "pos", "stage", "out", "pdve", "tb2", "base"))
        g_out = [g_out, sem("g_out_odd")]
        tb, t_ch, tab_ok, pad_ok = sem("tb"), sem("t_ch"), sem("tab_ok"), sem("pad_ok")
        e_in, e_xn, e_t, e_xhi, e_xlo, e_w1, e_h, e_y, e_yb, e_yo, e_out = (
            sem("e_" + n) for n in ("in", "xn", "t", "xhi", "xlo", "w1", "h", "y", "yb", "yo", "out"))
        e_out = [e_out, sem("e_out_odd")]
        e_in = [e_in] + [sem(f"e_in{n}") for n in range(1, RING)]

        def hold(eng, s, value):
            if not isinstance(value, int) or value > 0:
                eng.wait_ge(s, value)

        def settle(eng):
            eng.sem_inc(passed, 1)

        def layer(u):
            return (u % UNITS) // QUAD

        KINDS = {"all": (0, 1, 2), "first": (0,), "later": (1, 2), "inner": (0, 1), "last": (2,)}

        def made(q, kind, u):
            n = sum(1 for v in range(u + 1) if layer(v) in KINDS[kind])
            per = len(KINDS[kind]) * QUAD
            return n if isinstance(q, int) and q == 0 else q * per + n

        def gnn_steps(eng, step):
            for s in range(-3, 3):
                step(0, s, lambda u: u >= 0)
            with eng.Fori(0, QUADS - 1) as q:
                for s in range(3, UNITS + 3):
                    step(q, s, lambda u: True)
            for s in range(3, UNITS + 3):
                step(QUADS - 1, s, lambda u: u < UNITS)

        def graph0(q, u):
            return q * (QUAD * GR) + (u // UNITS) * QUAD * GR + (u % QUAD) * GR

        def gate_steps(eng, step):
            for s in range(-2, 3):
                step(s, s, 0)
            turns = (GROUPS - 5) // 4
            with eng.Fori(0, turns) as t:
                for s in range(3, 7):
                    step(t * 4 + s, s, t)
            for s in range(3 + 4 * turns, GROUPS + 2):
                step(s, s, 0)

        def expert_steps(eng, step):
            for s in range(-2, 3):
                step(s, s, 0)
            turns = (SGROUPS - 5) // RING
            with eng.Fori(0, turns) as t:
                for s in range(3, RING + 3):
                    step(t * RING + s, s, t)
            for s in range(3 + RING * turns, SGROUPS + 1):
                step(s, s, 0)

        def landed(t, per_turn, n, ways):
            return t * (per_turn // ways * GR * 16) + (n // ways + 1) * (GR * 16)

        def inside(s, n):
            return not isinstance(s, int) or 0 <= s < n

        block = ctx.enter_context(nc.Block())

        @block.sync
        def _(sp):
            sp.dma_start(wraw[:, 0:3, :], w_ih.rearrange("(g p) e -> p g e", p=P)).then_inc(w_in, 16)
            sp.dma_start(wraw[:, 3:6, :], w_hh.rearrange("(g p) e -> p g e", p=P)).then_inc(w_in, 16)
            sp.dma_start(wraw[:, 6:9, :], W.rearrange("l d e -> d l e")).then_inc(w_in, 16)
            xv = x.rearrange("g n c -> n g c")
            av = adj.rearrange("g s t -> s g t")
            with sp.Fori(0, GROUPS) as g:
                sp.dma_start(xres[:, bass.ds(g * GR, GR), :], xv[:, bass.ds(g * GR, GR), :]).then_inc(data_in, 16)
                sp.dma_start(adj_i[:, bass.ds(g * GR, GR), :], av[:, bass.ds(g * GR, GR), :]).then_inc(data_in, 16)
                sp.wait_ge(data_in, g * 32 + 32)
                settle(sp)
            sp.dma_start(w1raw[:], W1[:, :]).then_inc(ffn_in, 16)
            sp.dma_start(wd_sb[:].rearrange("p (e k c) -> p e k c", e=E, k=KC),
                         Wd.rearrange("e (k p) c -> p e k c", p=P)).then_inc(ffn_in, 16)
            sp.dma_start(wg_sb[:], Wg.rearrange("(k p) e -> p k e", p=P)).then_inc(ffn_in, 16)
            sp.dma_start(b1c[:], b1.rearrange("(k p) -> p k", p=P), allow_slow_non_contiguous=True).then_inc(ffn_in, 16)
            sp.dma_start(bd_bc[:], bd.rearrange("e c -> (e c)").partition_broadcast(P)).then_inc(ffn_in, 16)
            for j in range(GR):
                sp.dma_start(bg_bc[:, j, :], bg.partition_broadcast(P)).then_inc(ffn_in, 16)

            sp.wait_ge(g_out[0], GROUPS // 2 * GR * 16)
            sp.wait_ge(g_out[1], GROUPS // 2 * GR * 16)
            sp.wait_ge(pad_ok, (E + 1) * 16)
            sp.wait_ge(tab_ok, 1)
            def load_rows(group, b):
                for j in range(GR):
                    start = sp.value_load(row_tab[0:1, bass.ds(group * GR + j, 1)], min_val=0, max_val=E * REGION)
                    sp.dma_start(rows[:, b, j, :], sorted_rows[bass.ds(start, P), :]).then_inc(e_in[b], 16)

            for b in range(RING):
                load_rows(b, b)
            with sp.Fori(0, SGROUPS // RING - 1) as t:
                for b in range(RING):
                    sp.wait_ge(e_out[b % 2], landed(t, RING, b, 2))
                    load_rows(t * RING + RING + b, b)
            sp.wait_ge(e_out[0], SLOTS // 2 * 16)
            sp.wait_ge(e_out[1], SLOTS // 2 * 16)

        @block.gpsimd
        def _(pool):
            nc.gpsimd.memset(ident[:], 0.0).then_inc(c_id, 1)
            nc.gpsimd.memset(ones[:], 1.0).then_inc(c_msk, 1)
            pool.wait_ge(c_id, 1)
            nc.gpsimd.affine_select(out=ident[:], in_=ident[:], compare_op=ALU.not_equal, fill=1.0, base=0,
                                    pattern=[[-1, P]], channel_multiplier=1).then_inc(c_id, 1)
            pool.wait_ge(c_msk, 1)
            nc.gpsimd.affine_select(out=before[:], in_=ones[:], compare_op=ALU.is_gt, fill=0.0, base=0,
                                    pattern=[[1, P]], channel_multiplier=-1).then_inc(c_msk, 1)
            nc.gpsimd.memset(half[:], -0.5).then_inc(c_gp, 1)
            nc.gpsimd.iota(ids[:], [[P, GRAPHS]], base=0, channel_multiplier=1).then_inc(c_gp, 1)
            nc.gpsimd.iota(iot[:], [[0, GR], [-1, E]], base=E, channel_multiplier=0).then_inc(c_gp, 1)
            nc.gpsimd.iota(ecap_i[:], [[1, E]], base=0, channel_multiplier=0).then_inc(c_gp, 1)
            nc.gpsimd.iota(slot_i[:], [[1, SLOTS], [0, E]], base=0, channel_multiplier=0).then_inc(c_gp, 1)
            nc.gpsimd.iota(tri_i[:], [[1, E], [-1, E]], base=0, channel_multiplier=0).then_inc(c_gp, 1)
            nc.gpsimd.iota(part_i[:], [[0, 1]], base=0, channel_multiplier=1).then_inc(c_gp, 1)
            nc.gpsimd.memset(padrow[:, 0:TOKEN], 0.0).then_inc(c_gp, 1)
            nc.gpsimd.iota(padrow[:, TOKEN:ROW].bitcast(i32), [[0, 1]], base=NOBODY, channel_multiplier=1).then_inc(c_gp, 1)
            pool.wait_ge(c_gp, 9)

            def step(q, s, exists):
                u = s + 3
                if exists(u) and layer(u) == 0:
                    g = u % QUAD
                    hold(pool, mv_ok, made(q, "first", u))
                    settle(pool)
                    nc.gpsimd.tensor_scalar(rstd[:, g, :], mv[:, g, :, 1], EPS, None, ALU.add).then_inc(var_ok, 1)
                    hold(pool, var_ok, made(q, "first", u))
                    settle(pool)
                    nc.gpsimd.tensor_tensor(rstd[:, g, :], rstd[:, g, :], half[:], ALU.pow).then_inc(rstd_ok, 1)
                u = s + 1
                if exists(u) and layer(u) == 0:
                    hold(pool, x0hi_ok, made(q, "first", u))
                    settle(pool)
                    nc.gpsimd.tensor_tensor(hn_lo[:, u % 2, :], xn[:, u % QUAD, :],
                                            hn_hi[:, u % 2, :].bitcast(fp32), ALU.subtract).then_inc(x0lo_ok, 1)
                u = s - 1
                if exists(u):
                    g, b = u % QUAD, u % 2
                    hold(pool, n_ok, made(q, "all", u))
                    settle(pool)
                    nc.gpsimd.tensor_tensor(diff[:, b, :], hT[:, g, :], n_sb[:, b, :], ALU.subtract).then_inc(diff_ok, 1)
                    hold(pool, diff_ok, made(q, "all", u))
                    settle(pool)
                    nc.gpsimd.tensor_tensor(diff[:, b, :], z_sb[:, g, :], diff[:, b, :], ALU.mult).then_inc(zd_ok, 1)
                u = s - 2
                if exists(u) and layer(u) < LAYERS - 1:
                    g = u % QUAD
                    hold(pool, hthi_ok, made(q, "inner", u))
                    settle(pool)
                    nc.gpsimd.tensor_tensor(hT_lo[:, g, :], hT[:, g, :], hT_hi[:, g, :].bitcast(fp32),
                                            ALU.subtract).then_inc(htlo_ok, 1)

            gnn_steps(pool, step)

            def step(s, c, t):
                if inside(s + 2, GROUPS):
                    b = (c + 2) % 4
                    hold(pool, g_mv, s + 3)
                    settle(pool)
                    nc.gpsimd.tensor_scalar(rstd[:, b, :], mv[:, b, :, 1], EPS, None, ALU.add).then_inc(g_var, 1)
                    hold(pool, g_var, s + 3)
                    settle(pool)
                    nc.gpsimd.tensor_tensor(rstd[:, b, :], rstd[:, b, :], half[:], ALU.pow).then_inc(g_rstd, 1)
                if inside(s - 1, GROUPS):
                    b, b4 = (c - 1) % 2, (c - 1) % 4
                    hold(pool, g_out[b], landed(t, 4, c - 3, 2))
                    settle(pool)
                    nc.gpsimd.tensor_copy(stage[:, b, :, 0:P], xres[:, bass.ds((s - 1) * GR, GR), :]).then_inc(g_stage, 1)
                    nc.gpsimd.tensor_copy(stage[:, b, :, MEAN:MEAN + 1], mv[:, b4, :, 0:1]).then_inc(g_stage, 1)
                    nc.gpsimd.tensor_copy(stage[:, b, :, RSTD:RSTD + 1], rstd[:, b4, :].unsqueeze(2)).then_inc(g_stage, 1)
                    nc.gpsimd.tensor_copy(stage[:, b, :, TOKEN:ROW].bitcast(i32),
                                          ids[:, bass.ds((s - 1) * GR, GR)].unsqueeze(2)).then_inc(g_stage, 1)
                    pool.wait_ge(g_stage, s * 4)
                    pool.wait_ge(g_prob, s)
                    pool.wait_ge(g_pos, s)
                    settle(pool)
                    for j in range(GR):
                        nc.gpsimd.indirect_dma_start(
                            out=sorted_rows, out_offset=bass.IndirectOffsetOnAxis(ap=pos[:, b, j:j + 1], axis=0),
                            in_=stage[:, b, j, :], in_offset=None).then_inc(g_out[b], 16)

            gate_steps(pool, step)

            pool.wait_ge(tb, 4)
            for e in range(E + 1):
                nc.gpsimd.indirect_dma_start(
                    out=sorted_rows, out_offset=bass.IndirectOffsetOnAxis(ap=padi[:, e:e + 1], axis=0),
                    in_=padrow[:], in_offset=None).then_inc(pad_ok, 16)

            def step(s, c, t):
                if inside(s - 1, SGROUPS):
                    b = (c - 1) % 2
                    pool.wait_ge(e_yo, s * GR)
                    settle(pool)
                    for j in range(GR):
                        nc.gpsimd.indirect_dma_start(
                            out=h_out, out_offset=bass.IndirectOffsetOnAxis(
                                ap=rows[:, (c - 1) % RING, j, TOKEN:ROW].bitcast(u32), axis=0),
                            in_=yo[:, b, j, :], in_offset=None, bounds_check=TOK - 1, oob_is_err=False).then_inc(e_out[b], 16)

            expert_steps(pool, step)

        @block.tensor
        def _(pe):
            def three(o, w_hi, w_lo, x_hi, x_lo, start, stop):
                nc.tensor.matmul(o, w_hi, x_hi, start=start, stop=False)
                nc.tensor.matmul(o, w_hi, x_lo, start=False, stop=False)
                return nc.tensor.matmul(o, w_lo, x_hi, start=False, stop=stop)

            pe.wait_ge(c_id, 2)
            pe.wait_ge(w_in, 48)
            for k, o in ((0, pR), (1, pZ), (2, pGH)):
                for j in range(3):
                    last = nc.tensor.transpose(o[:, j * P:(j + 1) * P], wraw[:, 3 * k + j, :], ident[:])
                last.then_inc(wt_ps, 1)
            pe.wait_ge(wt_sb, 2)
            for l, o in enumerate((pGI, pAG, pF)):
                nc.tensor.matmul(o[:, 0:3 * P], wT[:, 3 + l, :], wT[:, 0:3, :].rearrange("p g e -> p (g e)"),
                                 start=True, stop=True).then_inc(wf_ps, 1)
            pe.wait_ge(whi_done, LAYERS + 1)
            pe.wait_ge(wlo_done, LAYERS + 1)

            def step(q, s, exists):
                g, b = s % QUAD, s % 2
                if exists(s):
                    if layer(s) == 0:
                        hold(pe, h0hi_ok, made(q, "first", s))
                        hold(pe, h0lo_ok, made(q, "first", s))
                    else:
                        hold(pe, hthi_ok, made(q, "inner", s - 4))
                        hold(pe, htlo_ok, made(q, "inner", s - 4))
                    for k, (o, freed) in enumerate(((pR, r_ok), (pZ, z_ok), (pGH, rhn_ok))):
                        hold(pe, freed, made(q, "all", s - 1))
                        w = slice(k * P, (k + 1) * P)
                        last = three(o[:], whh_hi[:, w], whh_lo[:, w], hT_hi[:, g, :], hT_lo[:, g, :],
                                     start=True, stop=(k == 2))
                    last.then_inc(hh_ps, 1)
                u = s - 3
                if exists(u) and layer(u) == LAYERS - 1:
                    hold(pe, h_ok, made(q, "all", u))
                    hold(pe, x1_ok, made(q, "last", u - 1))
                    for j in range(GR):
                        last = nc.tensor.transpose(pF[:, j * P:(j + 1) * P], hT[:, u % QUAD, j * P:(j + 1) * P], ident[:])
                    last.then_inc(f_ps, 1)
                u = s + 1
                if exists(u):
                    if layer(u) == 0:
                        hold(pe, xn_ok, made(q, "first", u))
                        src = xn
                    else:
                        hold(pe, h_ok, made(q, "all", u - 4))
                        src = hT
                    for j in range(GR):
                        last = nc.tensor.transpose(pT[:, j * P:(j + 1) * P], src[:, u % QUAD, j * P:(j + 1) * P], ident[:])
                    last.then_inc(t_ps, 1)
                if exists(s):
                    hold(pe, aghi_ok, made(q, "all", s))
                    hold(pe, aglo_ok, made(q, "all", s))
                    for k, (o, done) in enumerate(((pR, r_ps), (pZ, z_ps), (pGI, in_ps))):
                        if k == 2:
                            hold(pe, cand_ok, made(q, "all", s - 1))
                        w = slice(k * P, (k + 1) * P)
                        three(o[:], wf_hi[:, layer(s), w], wf_lo[:, layer(s), w], ag_hi[:, b, :], ag_lo[:, b, :],
                              start=(k == 2), stop=True).then_inc(done, 1)
                if exists(u):
                    if layer(u) == 0:
                        hold(pe, adj_ok, made(q, "first", u))
                        hold(pe, x0hi_ok, made(q, "first", u))
                        hold(pe, x0lo_ok, made(q, "first", u))
                    else:
                        hold(pe, hnhi_ok, made(q, "later", u))
                        hold(pe, hnlo_ok, made(q, "later", u))
                    for j in range(GR):
                        c = slice(j * P, (j + 1) * P)
                        nc.tensor.matmul(pAG[:, c], hn_hi[:, u % 2, c], A[:, u % QUAD, c], start=True, stop=False)
                        last = nc.tensor.matmul(pAG[:, c], hn_lo[:, u % 2, c], A[:, u % QUAD, c], start=False, stop=True)
                    last.then_inc(ag_ps, 1)

            gnn_steps(pe, step)
            pe.wait_ge(x1_ok, GROUPS)

            HB = (pR, pZ, pGH, pGI)

            def hidden(xb, done):
                for k in range(KC):
                    w = slice(k * P, (k + 1) * P)
                    three(HB[k][:], w1_hi[:, w], w1_lo[:, w], hT_hi[:, xb, :], hT_lo[:, xb, :],
                          start=True, stop=True).then_inc(done, 1)

            def step(s, c, t):
                if inside(s, GROUPS):
                    if c == 0:
                        pe.wait_ge(w1_hi_done, 1)
                        pe.wait_ge(w1_lo_done, 1)
                    pe.wait_ge(g_xhi, s + 1)
                    pe.wait_ge(g_xlo, s + 1)
                    hold(pe, g_h, s * KC)
                    hidden(c % 2, g_w1)
                if inside(s - 1, GROUPS):
                    b = (c - 1) % 2
                    pe.wait_ge(g_oh, s)
                    hold(pe, g_pos, s - 1)
                    for j in range(GR):
                        o = pF[:, j * E:(j + 1) * E]
                        nc.tensor.matmul(o, before[:], oh[:, b, j, :], start=True, stop=(j == 0))
                        for i in range(j):
                            nc.tensor.matmul(o, ones[:], oh[:, b, i, :], start=False, stop=(i == j - 1))
                    o = pF[:, GR * E:(GR + 1) * E]
                    for i in range(GR):
                        last = nc.tensor.matmul(o, ones[:], oh[:, b, i, :], start=(i == 0), stop=(i == GR - 1))
                    last.then_inc(g_rk, 1)
                if inside(s + 1, GROUPS):
                    b4 = (c + 1) % 4
                    pe.wait_ge(g_xn, s + 2)
                    for j in range(GR):
                        last = nc.tensor.transpose(pT[:, j * P:(j + 1) * P], xn[:, b4, j * P:(j + 1) * P], ident[:])
                    last.then_inc(g_t, 1)
                if inside(s, GROUPS):
                    pe.wait_ge(g_h, (s + 1) * KC)
                    hold(pe, g_sh, s)
                    for j in range(GR):
                        for k in range(KC):
                            last = nc.tensor.matmul(pAG[:, j * E:(j + 1) * E], HT[:, c % 2, k, j * P:(j + 1) * P],
                                                    wg_sb[:, k, :], start=(k == 0), stop=(k == KC - 1))
                    last.then_inc(g_lg, 1)

            pe.wait_ge(ffn_in, 16 * (5 + GR))
            gate_steps(pe, step)

            pe.wait_ge(tab_ok, 1)

            def step(s, c, t):
                if inside(s, SGROUPS):
                    pe.wait_ge(e_xhi, s + 1)
                    pe.wait_ge(e_xlo, s + 1)
                    hold(pe, e_h, s * KC)
                    hidden(c % 2, e_w1)
                if inside(s + 1, SGROUPS):
                    b4 = (c + 1) % 2
                    pe.wait_ge(e_xn, (s + 2) * GR)
                    for j in range(GR):
                        last = nc.tensor.transpose(pT[:, j * P:(j + 1) * P], xn[:, b4, j * P:(j + 1) * P], ident[:])
                    last.then_inc(e_t, 1)
                if inside(s - 1, SGROUPS):
                    b = (c - 1) % 2
                    o = (pAG, pF)[b]
                    pe.wait_ge(e_h, s * KC)
                    hold(pe, e_yb, (s - 2) * GR)
                    for j in range(GR):
                        at = pe.value_load(wd_tab[0:1, bass.ds((s - 1) * GR + j, 1)], min_val=0,
                                           max_val=(E - 1) * KC * P)
                        for k in range(KC):
                            last = nc.tensor.matmul(o[:, j * P:(j + 1) * P], HT[:, b, k, j * P:(j + 1) * P],
                                                    wd_sb[:, bass.ds(at + k * P, P)],
                                                    start=(k == 0), stop=(k == KC - 1))
                    last.then_inc(e_y, 1)

            expert_steps(pe, step)

        @block.scalar
        def _(act):
            act.dma_start(bi[:], b_ih.rearrange("(k p) -> p k", p=P), allow_slow_non_contiguous=True).then_inc(b_in, 16)
            act.dma_start(bh[:], b_hh.rearrange("(k p) -> p k", p=P), allow_slow_non_contiguous=True).then_inc(b_in, 16)
            act.wait_ge(wt_ps, 1)
            nc.scalar.activation(wT[:, 0:3, :].rearrange("p g e -> p (g e)"), pR[:, 0:3 * P], ACT.Copy).then_inc(wt_sb, 1)
            act.wait_ge(wt_ps, 3)
            nc.scalar.activation(wT[:, 3:6, :].rearrange("p g e -> p (g e)"), pGH[:, 0:3 * P], ACT.Copy).then_inc(wt_sb, 1)
            nc.scalar.activation(whh_hi[:], pZ[:, 0:3 * P], ACT.Copy).then_inc(whi_done, 1)
            for l, o in enumerate((pGI, pAG, pF)):
                act.wait_ge(wf_ps, l + 1)
                nc.scalar.activation(wf_hi[:, l, :], o[:, 0:3 * P], ACT.Copy).then_inc(whi_done, 1)
            act.wait_ge(c_dv, 1)

            def step(q, s, exists):
                b = s % 2
                if exists(s):
                    hold(act, ag_ps, made(q, "all", s))
                    nc.scalar.activation(ag_hi[:, b, :], pAG[:], ACT.Copy).then_inc(aghi_ok, 1)
                u = s - 1
                if exists(u):
                    hold(act, cand_ok, made(q, "all", u))
                    nc.scalar.activation(n_sb[:, u % 2, :], cand[:, u % 2, :], ACT.Tanh, bias=bi[:, 2:3]).then_inc(n_ok, 1)
                u = s + 1
                if exists(u) and layer(u) == 0:
                    hold(act, xn_ok, made(q, "first", u))
                    nc.scalar.activation(hn_hi[:, u % 2, :], xn[:, u % QUAD, :], ACT.Copy).then_inc(x0hi_ok, 1)
                u = s - 2
                if exists(u) and layer(u) < LAYERS - 1:
                    hold(act, h_ok, made(q, "all", u))
                    nc.scalar.activation(hT_hi[:, u % QUAD, :], hT[:, u % QUAD, :], ACT.Copy).then_inc(hthi_ok, 1)
                u = s + 1
                if exists(u):
                    hold(act, t_ps, made(q, "all", u))
                    if layer(u) == 0:
                        nc.scalar.activation(hT[:, u % QUAD, :], pT[:], ACT.Copy).then_inc(h0_ok, 1)
                        nc.scalar.activation(hT_hi[:, u % QUAD, :], pT[:], ACT.Copy).then_inc(h0hi_ok, 1)
                    else:
                        nc.scalar.activation(hn_hi[:, u % 2, :], pT[:], ACT.Copy).then_inc(hnhi_ok, 1)
                if exists(s):
                    hold(act, r_ps, made(q, "all", s))
                    nc.scalar.activation(r_sb[:, b, :], pR[:], ACT.Sigmoid, bias=bsum[:, 0:1]).then_inc(r_ok, 1)
                    hold(act, z_ps, made(q, "all", s))
                    nc.scalar.activation(z_sb[:, s % QUAD, :], pZ[:], ACT.Sigmoid, bias=bsum[:, 1:2]).then_inc(z_ok, 1)

            gnn_steps(act, step)
            act.wait_ge(ffn_in, 16 * (5 + GR))
            nc.scalar.activation(w1_hi[:], w1raw[:], ACT.Copy).then_inc(w1_hi_done, 1)

            def gelus(hb, s, ready, done):
                for k in range(KC):
                    hold(act, ready, s * KC + k + 1)
                    nc.scalar.activation(HT[:, hb, k, :], HB[k][:], ACT.Gelu, bias=b1c[:, k:k + 1]).then_inc(done, 1)

            HB = (pR, pZ, pGH, pGI)

            def step(s, c, t):
                if inside(s - 1, GROUPS):
                    b = (c - 1) % 2
                    act.wait_ge(g_sh, s)
                    nc.scalar.activation(th[:, b, :, :], sh[:, b, :, :], ACT.Tanh, scale=0.5).then_inc(g_th, 1)
                if inside(s, GROUPS):
                    gelus(c % 2, s, g_w1, g_h)
                if inside(s + 1, GROUPS):
                    act.wait_ge(g_t, s + 2)
                    nc.scalar.activation(hT_hi[:, (c + 1) % 2, :], pT[:], ACT.Copy).then_inc(g_xhi, 1)

            gate_steps(act, step)

            def step(s, c, t):
                if inside(s, SGROUPS):
                    hold(act, e_y, s - 1)
                    gelus(c % 2, s, e_w1, e_h)
                if inside(s + 1, SGROUPS):
                    act.wait_ge(e_t, s + 2)
                    nc.scalar.activation(hT_hi[:, (c + 1) % 2, :], pT[:], ACT.Copy).then_inc(e_xhi, 1)

            expert_steps(act, step)

        @block.vector
        def _(dve):
            tt, ts = nc.vector.tensor_tensor, nc.vector.tensor_scalar
            stt, red = nc.vector.scalar_tensor_tensor, nc.vector.tensor_reduce
            dve.wait_ge(whi_done, 1)
            tt(whh_lo[:], pZ[:, 0:3 * P], whh_hi[:].bitcast(fp32), ALU.subtract).then_inc(wlo_done, 1)
            dve.wait_ge(b_in, 32)
            tt(bsum[:], bi[:], bh[:], ALU.add).then_inc(c_dv, 1)
            for l, o in enumerate((pGI, pAG, pF)):
                dve.wait_ge(whi_done, l + 2)
                tt(wf_lo[:, l, :], o[:, 0:3 * P], wf_hi[:, l, :].bitcast(fp32), ALU.subtract).then_inc(wlo_done, 1)
            dve.wait_ge(c_gp, 9)

            def row_stats(b, graph, bn, bn_at, mv_done):
                for j in range(GR):
                    last = nc.vector.bn_stats(stats[:, b, j, :], xres[:, graph + j, :] if isinstance(graph, int)
                                              else xres[:, bass.ds(graph + j, 1), :].rearrange("p o c -> p (o c)"))
                last.then_inc(bn, 1)
                hold(dve, bn, bn_at)
                settle(dve)
                for j in range(GR):
                    last = nc.vector.bn_aggr(mv[:, b, j, :], stats[:, b, j, :])
                last.then_inc(mv_done, 1)

            def normalise(b, graph, done):
                for j in range(GR):
                    last = ts(xn[:, b, j * P:(j + 1) * P],
                              xres[:, graph + j, :] if isinstance(graph, int)
                              else xres[:, bass.ds(graph + j, 1), :].rearrange("p o c -> p (o c)"),
                              mv[:, b, j, 0:1], rstd[:, b, j:j + 1], ALU.subtract, ALU.mult)
                last.then_inc(done, 1)

            def step(q, s, exists):
                b = s % 2
                if exists(s):
                    hold(dve, aghi_ok, made(q, "all", s))
                    tt(ag_lo[:, b, :], pAG[:], ag_hi[:, b, :].bitcast(fp32), ALU.subtract).then_inc(aglo_ok, 1)
                u = s - 2
                if exists(u):
                    hold(dve, zd_ok, made(q, "all", u))
                    tt(hT[:, u % QUAD, :], n_sb[:, u % 2, :], diff[:, u % 2, :], ALU.add).then_inc(h_ok, 1)
                u = s + 2
                if exists(u) and layer(u) == 0:
                    hold(dve, rstd_ok, made(q, "first", u))
                    normalise(u % QUAD, graph0(q, u), xn_ok)
                u = s + 3
                if exists(u) and layer(u) == 0:
                    hold(dve, data_in, made(q, "first", u) * 32)
                    row_stats(u % QUAD, graph0(q, u), bn_ok, made(q, "first", u), mv_ok)
                    ts(A[:, u % QUAD, :].rearrange("p (g n) -> p g n", g=GR),
                       adj_i[:, bass.ds(graph0(q, u), GR), :], 0, None, ALU.not_equal).then_inc(adj_ok, 1)
                u = s + 1
                if exists(u):
                    if layer(u) == 0:
                        hold(dve, h0hi_ok, made(q, "first", u))
                        tt(hT_lo[:, u % QUAD, :], pT[:], hT_hi[:, u % QUAD, :].bitcast(fp32), ALU.subtract).then_inc(h0lo_ok, 1)
                    else:
                        hold(dve, hnhi_ok, made(q, "later", u))
                        tt(hn_lo[:, u % 2, :], pT[:], hn_hi[:, u % 2, :].bitcast(fp32), ALU.subtract).then_inc(hnlo_ok, 1)
                u = s - 3
                if exists(u) and layer(u) == LAYERS - 1:
                    hold(dve, f_ps, made(q, "last", u))
                    gx = xres[:, bass.ds(graph0(q, u), GR), :]
                    tt(gx, pF[:].rearrange("p (g n) -> p g n", g=GR), gx, ALU.add).then_inc(x1_ok, 1)
                if exists(s):
                    hold(dve, r_ok, made(q, "all", s))
                    stt(cand[:, b, :], pGH[:], bh[:, 2:3], r_sb[:, b, :], ALU.add, ALU.mult).then_inc(rhn_ok, 1)
                    hold(dve, in_ps, made(q, "all", s))
                    hold(dve, rhn_ok, made(q, "all", s))
                    tt(cand[:, b, :], pGI[:], cand[:, b, :], ALU.add).then_inc(cand_ok, 1)

            gnn_steps(dve, step)

            dve.wait_ge(w1_hi_done, 1)
            tt(w1_lo[:], w1raw[:], w1_hi[:].bitcast(fp32), ALU.subtract).then_inc(w1_lo_done, 1)
            nc.vector.tensor_copy(rev[:].rearrange("p g e -> p (g e)"), iot[:]).then_inc(tb, 1)
            ts(ecap[:], ecap_i[:], float(REGION), None, ALU.mult).then_inc(tb, 1)
            ts(base[:], ecap_i[:], float(REGION), None, ALU.mult).then_inc(tb, 1)
            dve.wait_ge(x1_ok, GROUPS)
            dve.wait_ge(tb, 3)

            ROUTE_A, ROUTE_B, SOFT = 4, 3, 4

            def step(s, c, t):
                here = inside(s - 1, GROUPS)
                b = (c - 1) % 2
                if here:
                    dve.wait_ge(g_lg, s)
                    n = (s - 1) * ROUTE_A
                    tt(lg[:, b, :, :], pAG[:, 0:GR * E].rearrange("p (g e) -> p g e", g=GR), bg_bc[:], ALU.add).then_inc(g_dve, 1)
                    dve.wait_ge(g_dve, n + 1)
                    red(mx[:, b, :], lg[:, b, :, :], AX.X, ALU.max).then_inc(g_dve, 1)
                    dve.wait_ge(g_dve, n + 2)
                    tt(sh[:, b, :, :], lg[:, b, :, :], mx[:, b, :].unsqueeze(2).to_broadcast([P, GR, E]),
                       ALU.subtract).then_inc(g_sh, 1)
                    dve.wait_ge(g_sh, s)
                    stt(mt[:, b, :, :], sh[:, b, :, :], 0.0, rev[:], ALU.is_ge, ALU.mult).then_inc(g_dve, 1)
                    dve.wait_ge(g_dve, n + 3)
                    red(mv8[:, b, :], mt[:, b, :, :], AX.X, ALU.max).then_inc(g_dve, 1)
                    dve.wait_ge(g_dve, n + 4)
                    tt(oh[:, b, :, :], mt[:, b, :, :], mv8[:, b, :].unsqueeze(2).to_broadcast([P, GR, E]),
                       ALU.is_equal).then_inc(g_oh, 1)
                if inside(s + 2, GROUPS):
                    b4 = (c + 2) % 4
                    hold(dve, g_stage, (s - 2) * 4 + 4)
                    row_stats(b4, (s + 2) * GR, g_bn, s + 3, g_mv)
                if here:
                    dve.wait_ge(g_th, s)
                    hold(dve, g_out[b], landed(t, 4, c - 3, 2))
                    m = (s - 1) * SOFT
                    ts(den[:, b, :, :], th[:, b, :, :], -1.0, 1.0, ALU.mult, ALU.add).then_inc(g_pdve, 1)
                    dve.wait_ge(g_pdve, m + 1)
                    nc.vector.reciprocal(num[:, b, :, :], den[:, b, :, :]).then_inc(g_pdve, 1)
                    dve.wait_ge(g_pdve, m + 2)
                    stt(ex[:, b, :, :], th[:, b, :, :], 1.0, num[:, b, :, :], ALU.add, ALU.mult).then_inc(g_pdve, 1)
                    dve.wait_ge(g_pdve, m + 3)
                    red(ssum[:, b, :], ex[:, b, :, :], AX.X, ALU.add).then_inc(g_pdve, 1)
                    dve.wait_ge(g_pdve, m + 4)
                    nc.vector.reciprocal(stage[:, b, :, PROB], ssum[:, b, :]).then_inc(g_prob, 1)
                if inside(s + 2, GROUPS):
                    dve.wait_ge(g_rstd, s + 3)
                    normalise((c + 2) % 4, (s + 2) * GR, g_xn)
                if inside(s + 1, GROUPS):
                    dve.wait_ge(g_xhi, s + 2)
                    tt(hT_lo[:, (c + 1) % 2, :], pT[:], hT_hi[:, (c + 1) % 2, :].bitcast(fp32), ALU.subtract).then_inc(g_xlo, 1)
                if here:
                    dve.wait_ge(g_rk, s)
                    m = (s - 1) * ROUTE_B
                    tt(rk[:, b, :, :], pF[:, 0:GR * E].rearrange("p (g e) -> p g e", g=GR),
                       base[:].unsqueeze(1).to_broadcast([P, GR, E]), ALU.add).then_inc(tb2, 1)
                    dve.wait_ge(tb2, m + 1)
                    tt(base[:], pF[:, GR * E:(GR + 1) * E], base[:], ALU.add).then_inc(base_ok, 1)
                    tt(rk[:, b, :, :], rk[:, b, :, :], oh[:, b, :, :], ALU.mult).then_inc(tb2, 1)
                    dve.wait_ge(tb2, m + 2)
                    red(posf[:, b, :], rk[:, b, :, :], AX.X, ALU.add).then_inc(tb2, 1)
                    dve.wait_ge(tb2, m + 3)
                    nc.vector.tensor_copy(pos[:, b, :], posf[:, b, :]).then_inc(g_pos, 1)
                    dve.wait_ge(base_ok, s)

            tb2, base_ok = g_tb2, g_base
            dve.wait_ge(ffn_in, 16 * (5 + GR))
            gate_steps(dve, step)

            chain = [0]

            def then(ins):
                chain[0] += 1
                ins.then_inc(t_ch, 1)
                dve.wait_ge(t_ch, chain[0])

            nc.vector.tensor_copy(part[:], part_i[:]).then_inc(t_ch, 1)
            chain[0] = 1
            dve.wait_ge(t_ch, 1)
            ts(padf[:, 0:E], base[:], part[:, 0:1], None, ALU.add).then_inc(t_ch, 1)
            ts(padf[:, E:E + 1], part[:], float(E * REGION), None, ALU.add).then_inc(t_ch, 1)
            chain[0] = 3
            dve.wait_ge(t_ch, 3)
            nc.vector.tensor_copy(padi[:], padf[:]).then_inc(tb, 1)
            then(tt(nf[:], base[0:1, :], ecap[0:1, :], ALU.subtract))
            then(ts(ni[:], nf[:], float(P - 1), None, ALU.add))
            then(ts(ni[:], ni[:], 7, None, ALU.arith_shift_right))
            then(nc.vector.tensor_copy(nblk[:], ni[:]))
            then(ts(tri[:], tri_i[:], 0.0, None, ALU.is_ge))
            then(tt(cumt[:], tri[:], nblk[:].unsqueeze(1).to_broadcast([1, E, E]), ALU.mult))
            then(red(cum[:], cumt[:], AX.X, ALU.add))
            then(ts(skip[:], nblk[:], float(-P), float(REGION), ALU.mult, ALU.add))
            then(nc.vector.tensor_copy(z_flat[:, 0:SLOTS * E], slot_i[:]))
            then(tt(le, slotf, cum[:].unsqueeze(1).to_broadcast([1, SLOTS, E]), ALU.is_ge))
            then(red(esum[:], le, AX.X, ALU.add))
            then(ts(esum[:], esum[:], float(E - 1), None, ALU.min))
            then(ts(wd_tab[:], esum[:], float(KC * P), None, ALU.mult))
            then(ts(bd_tab[:], esum[:], float(P), None, ALU.mult))
            then(tt(le, le, skip[:].unsqueeze(1).to_broadcast([1, SLOTS, E]), ALU.mult))
            then(red(rsum[:], le, AX.X, ALU.add))
            then(stt(rsum[:], slotf[:, :, 0], float(P), rsum[:], ALU.mult, ALU.add))
            then(ts(row_tab[:], rsum[:], float(E * REGION), None, ALU.min))
            nc.vector.tensor_copy(part[:], part_i[:]).then_inc(tab_ok, 1)

            def step(s, c, t):
                if inside(s + 2, SGROUPS):
                    b, r = (c + 2) % 2, (c + 2) % RING
                    dve.wait_ge(e_in[r], landed(t, RING, c + 2, RING))
                    hold(dve, e_t, s + 1)
                    for j in range(GR):
                        ts(xn[:, b, j * P:(j + 1) * P], rows[:, r, j, 0:P], rows[:, r, j, MEAN:MEAN + 1],
                           rows[:, r, j, RSTD:RSTD + 1], ALU.subtract, ALU.mult).then_inc(e_xn, 1)
                if inside(s + 1, SGROUPS):
                    dve.wait_ge(e_xhi, s + 2)
                    tt(hT_lo[:, (c + 1) % 2, :], pT[:], hT_hi[:, (c + 1) % 2, :].bitcast(fp32), ALU.subtract).then_inc(e_xlo, 1)
                if inside(s - 1, SGROUPS):
                    b, r = (c - 1) % 2, (c - 1) % RING
                    o = (pAG, pF)[b]
                    dve.wait_ge(e_y, s)
                    hold(dve, e_out[b], landed(t, RING, c - 3, 2))
                    for j in range(GR):
                        at = dve.value_load(bd_tab[0:1, bass.ds((s - 1) * GR + j, 1)], min_val=0, max_val=(E - 1) * P)
                        tt(yb[:, b, j, :], o[:, j * P:(j + 1) * P], bd_bc[:, bass.ds(at, P)], ALU.add).then_inc(e_yb, 1)
                    for j in range(GR):
                        dve.wait_ge(e_yb, (s - 1) * GR + j + 1)
                        stt(yo[:, b, j, :], yb[:, b, j, :], rows[:, r, j, PROB:PROB + 1], rows[:, r, j, 0:P],
                            ALU.mult, ALU.add).then_inc(e_yo, 1)

            expert_steps(dve, step)


_INS = ['x', 'adj', 'L0_gnn_weight', 'L0_gnn_w_ih', 'L0_gnn_w_hh', 'L0_gnn_b_ih', 'L0_gnn_b_hh',
        'L0_ffn_W1', 'L0_ffn_b1', 'L0_ffn_Wg', 'L0_ffn_bg', 'L0_ffn_Wd', 'L0_ffn_bd']


def kernel(**inputs):
    import numpy as _np
    import concourse.bacc as _bacc
    from concourse import mybir as _mybir
    from concourse.bass_utils import run_bass_kernel_spmd as _run

    nc = _bacc.Bacc("TRN2", target_bir_lowering=False, num_devices=1)
    arrays, args = {}, []
    for name in _INS:
        a = _np.ascontiguousarray(inputs[name])
        arrays[f"in_{name}_dram"] = a
        args.append(nc.dram_tensor(f"in_{name}_dram", a.shape, _mybir.dt.from_np(a.dtype), kind="ExternalInput").ap())
    shape = inputs['x'].shape
    args.append(nc.dram_tensor("out_0_dram", shape, _mybir.dt.float32, kind="ExternalOutput").ap())
    build(nc, *args)
    r = _run(nc, [arrays], core_ids=[0])
    return r.results[0]["out_0_dram"]
```

```python
import concourse.bass as bass
from concourse import mybir
from contextlib import ExitStack


fp32 = mybir.dt.float32
f32r = mybir.dt.float32r
bf16 = mybir.dt.bfloat16
i32 = mybir.dt.int32
u32 = mybir.dt.uint32
ALU = mybir.AluOpType
ACT = mybir.ActivationFunctionType
AX = mybir.AxisListType

P = 128
GR = 4
NT = GR * P
LAYERS = 3
QUAD = 4
UNITS = QUAD * LAYERS


def build(nc, x, adj, W, w_ih, w_hh, b_ih, b_hh, W1, b1, Wg, bg, Wd, bd, out):
    GRAPHS = x.shape[0]
    GROUPS = GRAPHS // GR
    QUADS = GROUPS // QUAD
    TOK = GRAPHS * P
    HID = W1.shape[1]
    KC = HID // P
    CT = P // KC
    E = Wd.shape[0]
    EPS = 1e-5
    REGION = TOK + P
    ROW = P + 4
    MEAN, RSTD, PROB, TOKEN = P, P + 1, P + 2, P + 3
    SLOTS = -(-((TOK + E * (P - 1)) // P) // GR) * GR
    SGROUPS = SLOTS // GR
    RING = 6
    NOBODY = 1 << 20

    h_out = out.rearrange("a n c -> (a n) c")
    sorted_rows = nc.dram_tensor("sorted_rows", ((E + 1) * REGION, ROW), fp32).ap()

    ctx = ExitStack()
    with ctx:
        def sb(name, shape, dt=fp32):
            return ctx.enter_context(nc.sbuf_tensor(name, shape, dt))

        def sem(name):
            return ctx.enter_context(nc.semaphore(name))

        ident = sb("ident", [P, P])
        half = sb("half", [P, GR])
        before = sb("before", [P, P], bf16)
        ones = sb("ones", [P, P], bf16)
        wraw = sb("wraw", [P, 9, P])
        wT = sb("wT", [P, 6, P])
        whh_hi, whh_lo = sb("whh_hi", [P, 3 * P], f32r), sb("whh_lo", [P, 3 * P], f32r)
        wf_hi, wf_lo = sb("wf_hi", [P, LAYERS, 3 * P], f32r), sb("wf_lo", [P, LAYERS, 3 * P], f32r)
        w1raw = sb("w1raw", [P, HID])
        w1_hi, w1_lo = sb("w1_hi", [P, HID], f32r), sb("w1_lo", [P, HID], f32r)
        b1c = sb("b1c", [P, KC])
        wg_sb = sb("wg_sb", [P, KC, CT])
        wd_sb = sb("wd_sb", [P, E * KC * P])
        bd_bc = sb("bd_bc", [P, E * P])
        bg_col = sb("bg_col", [P, 1])
        bi, bh = sb("bi", [P, 3]), sb("bh", [P, 3])
        bsum = sb("bsum", [P, 3])
        xrow = sb("xrow", [P, GRAPHS, ROW])
        xres = xrow[:, :, 0:P]
        adj_i = sb("adj_i", [P, GRAPHS, P], i32)
        A = sb("A", [P, QUAD, NT], f32r)
        hT = sb("hT", [P, QUAD, NT])
        hT_hi, hT_lo = sb("hT_hi", [P, QUAD, NT], f32r), sb("hT_lo", [P, QUAD, NT], f32r)
        hn_hi, hn_lo = sb("hn_hi", [P, 2, NT], f32r), sb("hn_lo", [P, 2, NT], f32r)
        ag_hi, ag_lo = sb("ag_hi", [P, 2, NT], f32r), sb("ag_lo", [P, 2, NT], f32r)
        r_sb, cand = sb("r_sb", [P, 2, NT]), sb("cand", [P, 2, NT])
        n_sb, diff = sb("n_sb", [P, 2, NT]), sb("diff", [P, 2, NT])
        z_sb = sb("z_sb", [P, QUAD, NT])
        xn = sb("xn", [P, QUAD, NT])
        stats = sb("stats", [P, QUAD, GR, 6])
        mv = sb("mv", [P, QUAD, GR, 2])
        ids = sb("ids", [P, GRAPHS], i32)
        stage = sb("stage", [P, 2, GR, ROW])
        lgT = sb("lgT", [P, NT])
        pick = sb("pick", [P, E])
        sh, mt = (sb(n, [P, 2, GR, E]) for n in ("sh", "mt"))
        oh = sb("oh", [P, 2, GR + 1, E], bf16)
        th, num, den, ex, rk = (sb(n, [P, 2, GR, E]) for n in ("th", "num", "den", "ex", "rk"))
        nw_v, nw_h, nw_a, nw_y = (sb(n, [P, 4 * GR]) for n in ("nw_v", "nw_h", "nw_a", "nw_y"))
        nw_i = sb("nw_i", [P, 4 * GR], i32)
        mx, mv8, ssum, posf = (sb(n, [P, 2, GR]) for n in ("mx", "mv8", "ssum", "posf"))
        pos = sb("pos", [P, 2, GR], u32)
        rev = sb("rev", [P, GR, E])
        ecap = sb("ecap", [P, E])
        base = sb("base", [P, E])
        iot = sb("iot", [P, GR * E], i32)
        ecap_i = sb("ecap_i", [P, E], i32)
        tri_i = sb("tri_i", [P, E, E], i32)
        tri = sb("tri", [P, E, E])
        slot_i, slot = sb("slot_i", [P, 1], i32), sb("slot", [P, 1])
        nf, nblk, cum, skip, le = (sb(n, [P, E]) for n in ("nf", "nblk", "cum", "skip", "le"))
        ni = sb("ni", [P, E], i32)
        cumt = sb("cumt", [P, E, E])
        esum, rsum = sb("esum", [P, 1]), sb("rsum", [P, 1])
        tab = sb("tab", [P, 3])
        tables = sb("tables", [1, 3, P], i32)
        row_tab, wd_tab, bd_tab = (tables[:, k, :] for k in range(3))
        pad_tab = sb("pad_tab", [1, E], i32)
        padrow = sb("padrow", [P, ROW])
        adj_f = adj_i[:, :, :].rearrange("p g n -> p (g n)").bitcast(fp32)
        HT = adj_f[:, 0:2 * KC * NT].rearrange("p (b k n) -> p b k n", b=2, k=KC)
        rows = adj_f[:, 2 * KC * NT:2 * KC * NT + RING * GR * ROW].rearrange(
            "p (b s r) -> p b s r", b=RING, s=GR)
        home = sb("home", [P, 2, GR], u32)
        yb = r_sb[:, :, :].rearrange("p b (s c) -> p b s c", s=GR)
        yo = cand[:, :, :].rearrange("p b (s c) -> p b s c", s=GR)

        bank = [ctx.enter_context(nc.psum_tensor(f"bank{i}", [P, NT], fp32)) for i in range(8)]
        pR, pZ, pGH, pGI, pAG, pT, pF, pX = bank

        w_in = sem("w_in")
        ffn_in = sem("ffn_in")
        padded = sem("padded")
        b_in = sem("b_in")
        data_in = sem("data_in")
        passed = sem("passed")
        c_id, c_msk, c_gp, c_dv = sem("c_id"), sem("c_msk"), sem("c_gp"), sem("c_dv")
        wt_ps, wt_sb, wf_ps = sem("wt_ps"), sem("wt_sb"), sem("wf_ps")
        whi_done, wlo_done = sem("whi_done"), sem("wlo_done")
        w1_hi_done, w1_lo_done = sem("w1_hi_done"), sem("w1_lo_done")
        hh_ps, r_ps, z_ps, in_ps, ag_ps, t_ps, f_ps = (
            sem(n) for n in ("hh_ps", "r_ps", "z_ps", "in_ps", "ag_ps", "t_ps", "f_ps"))
        aghi_ok, r_ok, z_ok, n_ok, hnhi_ok, hthi_ok, h0_ok, h0hi_ok, x0hi_ok = (
            sem(n) for n in ("aghi_ok", "r_ok", "z_ok", "n_ok", "hnhi_ok", "hthi_ok", "h0_ok", "h0hi_ok", "x0hi_ok"))
        aglo_ok, h_ok, hnlo_ok, h0lo_ok, rhn_ok, cand_ok, x1_ok, adj_ok = (
            sem(n) for n in ("aglo_ok", "h_ok", "hnlo_ok", "h0lo_ok", "rhn_ok", "cand_ok", "x1_ok", "adj_ok"))
        bn_ok, mv_ok, var_ok, rstd_ok, xn_ok = (sem(n) for n in ("bn_ok", "mv_ok", "var_ok", "rstd_ok", "xn_ok"))
        diff_ok, zd_ok, htlo_ok, x0lo_ok = (sem(n) for n in ("diff_ok", "zd_ok", "htlo_ok", "x0lo_ok"))
        g_bn, g_mv, g_rstd, g_xn, g_t, g_xhi, g_xlo, g_w1, g_h, g_lg, g_lgT, g_pick = (
            sem("g_" + n) for n in ("bn", "mv", "rstd", "xn", "t", "xhi", "xlo", "w1", "h", "lg", "lgT", "pick"))
        g_dve, g_sh, g_oh, g_th, g_rk, g_prob, g_pos, g_out, g_pdve, g_place, g_base = (
            sem("g_" + n) for n in ("dve", "sh", "oh", "th", "rk", "prob", "pos", "out", "pdve", "place", "base"))
        g_rows, g_tok, g_nw = sem("g_rows"), sem("g_tok"), sem("g_nw")
        g_out = [g_out, sem("g_out_odd")]
        tb, t_ch, tab_ps, tab_ok, pad_ok = sem("tb"), sem("t_ch"), sem("tab_ps"), sem("tab_ok"), sem("pad_ok")
        e_in, e_xn, e_t, e_xhi, e_xlo, e_w1, e_h, e_y, e_yb, e_yo, e_out = (
            sem("e_" + n) for n in ("in", "xn", "t", "xhi", "xlo", "w1", "h", "y", "yb", "yo", "out"))
        e_home = sem("e_home")
        e_out = [e_out, sem("e_out_odd")]
        e_in = [e_in] + [sem(f"e_in{n}") for n in range(1, RING)]

        def hold(eng, s, value):
            if not isinstance(value, int) or value > 0:
                eng.wait_ge(s, value)

        def settle(eng):
            eng.sem_inc(passed, 1)

        def layer(u):
            return (u % UNITS) // QUAD

        KINDS = {"all": (0, 1, 2), "first": (0,), "later": (1, 2), "inner": (0, 1), "last": (2,)}

        def made(q, kind, u):
            n = sum(1 for v in range(u + 1) if layer(v) in KINDS[kind])
            per = len(KINDS[kind]) * QUAD
            return n if isinstance(q, int) and q == 0 else q * per + n

        GATE_AFTER = {3: -6, 4: -5, 5: -4, 6: -3, UNITS - 2: -2, UNITS - 1: -1, UNITS: 0, UNITS + 1: 1}

        def gnn_steps(eng, step, gate):
            for s in range(-3, 3):
                step(0, s, lambda u: u >= 0)
            with eng.Fori(0, QUADS - 1) as q:
                for s in range(3, UNITS + 3):
                    step(q, s, lambda u: True)
            for s in range(3, UNITS + 3):
                step(QUADS - 1, s, lambda u: u < UNITS)
                if s in GATE_AFTER:
                    gate(GATE_AFTER[s], GATE_AFTER[s], 0)

        def ahead(s):
            return (3, 2) if s < 3 else (9, 6)

        def graph0(q, u):
            return q * (QUAD * GR) + (u // UNITS) * QUAD * GR + (u % QUAD) * GR

        def gate_steps(eng, step):
            for s in range(2, 5):
                step(s, s, 0)
            turns = (GROUPS - 9) // 4
            with eng.Fori(0, turns) as t:
                for s in range(5, 9):
                    step(t * 4 + s, s, t)
            for s in range(5 + 4 * turns, GROUPS + 3):
                step(s, s, 0)

        def expert_steps(eng, step):
            for s in range(-2, 3):
                step(s, s, 0)
            turns = (SGROUPS - 5) // RING
            with eng.Fori(0, turns) as t:
                for s in range(3, RING + 3):
                    step(t * RING + s, s, t)
            for s in range(3 + RING * turns, SGROUPS + 1):
                step(s, s, 0)

        def landed(t, per_turn, n, ways):
            return t * (per_turn // ways * GR * 16) + (n // ways + 1) * (GR * 16)

        def inside(s, n):
            return not isinstance(s, int) or 0 <= s < n

        FFN_LOADS = 16 * 6
        TABLE = 7
        block = ctx.enter_context(nc.Block())

        @block.sync
        def _(sp):
            sp.dma_start(wraw[:, 0:3, :], w_ih.rearrange("(g p) e -> p g e", p=P)).then_inc(w_in, 16)
            sp.dma_start(wraw[:, 3:6, :], w_hh.rearrange("(g p) e -> p g e", p=P)).then_inc(w_in, 16)
            sp.dma_start(wraw[:, 6:9, :], W.rearrange("l d e -> d l e")).then_inc(w_in, 16)
            xv = x.rearrange("g n c -> n g c")
            av = adj.rearrange("g s t -> s g t")
            with sp.Fori(0, GROUPS) as g:
                sp.dma_start(xres[:, bass.ds(g * GR, GR), :], xv[:, bass.ds(g * GR, GR), :]).then_inc(data_in, 16)
                sp.dma_start(adj_i[:, bass.ds(g * GR, GR), :], av[:, bass.ds(g * GR, GR), :]).then_inc(data_in, 16)
                sp.wait_ge(data_in, g * 32 + 32)
                settle(sp)
            sp.dma_start(w1raw[:], W1[:, :]).then_inc(ffn_in, 16)
            sp.dma_start(wd_sb[:].rearrange("p (e k c) -> p e k c", e=E, k=KC),
                         Wd.rearrange("e (k p) c -> p e k c", p=P)).then_inc(ffn_in, 16)
            sp.wait_ge(padded, 2)
            sp.dma_start(wg_sb[:, :, 0:E], Wg.rearrange("(k p) e -> p k e", p=P)).then_inc(ffn_in, 16)
            sp.dma_start(b1c[:], b1.rearrange("(k p) -> p k", p=P), allow_slow_non_contiguous=True).then_inc(ffn_in, 16)
            sp.dma_start(bd_bc[:], bd.rearrange("e c -> (e c)").partition_broadcast(P)).then_inc(ffn_in, 16)
            sp.dma_start(bg_col[0:E, :], bg.rearrange("(e o) -> e o", o=1)).then_inc(ffn_in, 16)

            sp.wait_ge(c_gp, 8)
            sp.dma_start(sorted_rows[E * REGION:E * REGION + P, :], padrow[:]).then_inc(pad_ok, 16)
            sp.wait_ge(tb, 4)
            for e in range(E):
                end = sp.value_load(pad_tab[0:1, e:e + 1], min_val=e * REGION, max_val=e * REGION + TOK)
                sp.dma_start(sorted_rows[bass.ds(end, P), :], padrow[:]).then_inc(pad_ok, 16)

            sp.wait_ge(tab_ok, 1)

            def starts(group, slots=range(GR)):
                return [sp.value_load(row_tab[0:1, bass.ds(group * GR + j, 1)], min_val=0, max_val=E * REGION)
                        for j in slots]

            def load_rows(start, b):
                for j in range(len(start)):
                    sp.dma_start(rows[:, b, j, :], sorted_rows[bass.ds(start[j], P), :]).then_inc(e_in[b], 16)

            first, second = starts(0, range(GR // 2)), starts(1, range(GR // 2))
            sp.wait_ge(g_out[0], GROUPS // 2 * GR * 16)
            sp.wait_ge(g_out[1], GROUPS // 2 * GR * 16)
            sp.wait_ge(pad_ok, (E + 1) * 16)
            load_rows(first, 0)
            load_rows(second, 1)
            for b in range(2, RING):
                load_rows(starts(b), b)
            with sp.Fori(0, SGROUPS // RING - 1) as t:
                for b in range(RING):
                    start = starts(t * RING + RING + b)
                    sp.wait_ge(e_out[b % 2], landed(t, RING, b, 2))
                    load_rows(start, b)
            sp.wait_ge(e_out[0], SLOTS // 2 * 16)
            sp.wait_ge(e_out[1], SLOTS // 2 * 16)

        @block.gpsimd
        def _(pool):
            nc.gpsimd.memset(ident[:], 0.0).then_inc(c_id, 1)
            nc.gpsimd.memset(ones[:], 1.0).then_inc(c_msk, 1)
            nc.gpsimd.memset(wg_sb[:], 0.0).then_inc(padded, 1)
            nc.gpsimd.memset(bg_col[:], 0.0).then_inc(padded, 1)
            nc.gpsimd.memset(oh[:, :, GR, :], 0.0).then_inc(c_msk, 1)
            pool.wait_ge(c_id, 1)
            nc.gpsimd.affine_select(out=ident[:], in_=ident[:], compare_op=ALU.not_equal, fill=1.0, base=0,
                                    pattern=[[-1, P]], channel_multiplier=1).then_inc(c_id, 1)
            pool.wait_ge(c_msk, 2)
            nc.gpsimd.affine_select(out=before[:], in_=ones[:], compare_op=ALU.is_gt, fill=0.0, base=0,
                                    pattern=[[1, P]], channel_multiplier=-1).then_inc(c_msk, 1)
            nc.gpsimd.memset(half[:], -0.5).then_inc(c_gp, 1)
            nc.gpsimd.iota(ids[:], [[P, GRAPHS]], base=0, channel_multiplier=1).then_inc(c_gp, 1)
            nc.gpsimd.iota(iot[:], [[0, GR], [-1, E]], base=E, channel_multiplier=0).then_inc(c_gp, 1)
            nc.gpsimd.iota(ecap_i[:], [[1, E]], base=0, channel_multiplier=0).then_inc(c_gp, 1)
            nc.gpsimd.iota(tri_i[:], [[1, E], [-1, E]], base=0, channel_multiplier=0).then_inc(c_gp, 1)
            nc.gpsimd.iota(slot_i[:], [[0, 1]], base=0, channel_multiplier=1).then_inc(c_gp, 1)
            nc.gpsimd.memset(padrow[:, 0:TOKEN], 0.0).then_inc(c_gp, 1)
            nc.gpsimd.memset(padrow[:, TOKEN:ROW], float(NOBODY)).then_inc(c_gp, 1)
            pool.wait_ge(c_gp, 8)

            def step(q, s, exists):
                u = s + 1
                if exists(u) and layer(u) == 0:
                    hold(pool, x0hi_ok, made(q, "first", u))
                    settle(pool)
                    nc.gpsimd.tensor_tensor(hn_lo[:, u % 2, :], xn[:, u % QUAD, :],
                                            hn_hi[:, u % 2, :].bitcast(fp32), ALU.subtract).then_inc(x0lo_ok, 1)
                u = s - 1
                if exists(u):
                    g, b = u % QUAD, u % 2
                    hold(pool, n_ok, made(q, "all", u))
                    settle(pool)
                    nc.gpsimd.tensor_tensor(diff[:, b, :], hT[:, g, :], n_sb[:, b, :], ALU.subtract).then_inc(diff_ok, 1)
                    hold(pool, diff_ok, made(q, "all", u))
                    settle(pool)
                    nc.gpsimd.tensor_tensor(diff[:, b, :], z_sb[:, g, :], diff[:, b, :], ALU.mult).then_inc(zd_ok, 1)
                u = s - 2
                if exists(u) and layer(u) < LAYERS - 1:
                    g = u % QUAD
                    hold(pool, hthi_ok, made(q, "inner", u))
                    settle(pool)
                    nc.gpsimd.tensor_tensor(hT_lo[:, g, :], hT[:, g, :], hT_hi[:, g, :].bitcast(fp32),
                                            ALU.subtract).then_inc(htlo_ok, 1)
                u = s + ahead(s)[0]
                if exists(u) and layer(u) == 0:
                    var = mv[:, u % QUAD, :, 1]
                    hold(pool, mv_ok, made(q, "first", u))
                    settle(pool)
                    nc.gpsimd.tensor_scalar(var, var, EPS, None, ALU.add).then_inc(var_ok, 1)
                    hold(pool, var_ok, made(q, "first", u))
                    settle(pool)
                    nc.gpsimd.tensor_tensor(var, var, half[:], ALU.pow).then_inc(rstd_ok, 1)

            def gate_step(s, c, t):
                if inside(s - 3, GROUPS):
                    b = (c - 3) % 2
                    pool.wait_ge(g_rows, s - 2)
                    pool.wait_ge(g_pos, s - 2)
                    settle(pool)
                    for j in range(GR):
                        nc.gpsimd.indirect_dma_start(
                            out=sorted_rows, out_offset=bass.IndirectOffsetOnAxis(ap=pos[:, b, j:j + 1], axis=0),
                            in_=stage[:, b, j, :], in_offset=None).then_inc(g_out[b], 16)

            gnn_steps(pool, step, gate_step)
            gate_steps(pool, gate_step)

            def step(s, c, t):
                if inside(s - 1, SGROUPS):
                    b = (c - 1) % 2
                    pool.wait_ge(e_home, s)
                    for j in range(GR):
                        pool.wait_ge(e_yo, (s - 1) * GR + j + 1)
                        settle(pool)
                        nc.gpsimd.indirect_dma_start(
                            out=h_out, out_offset=bass.IndirectOffsetOnAxis(
                                ap=home[:, b, j:j + 1], axis=0),
                            in_=yo[:, b, j, :], in_offset=None, bounds_check=TOK - 1, oob_is_err=False).then_inc(e_out[b], 16)

            expert_steps(pool, step)

        @block.tensor
        def _(pe):
            def three(o, w_hi, w_lo, x_hi, x_lo, start, stop):
                nc.tensor.matmul(o, w_hi, x_hi, start=start, stop=False)
                nc.tensor.matmul(o, w_hi, x_lo, start=False, stop=False)
                return nc.tensor.matmul(o, w_lo, x_hi, start=False, stop=stop)

            pe.wait_ge(c_id, 2)
            pe.wait_ge(w_in, 48)
            for k, o in ((0, pR), (1, pZ), (2, pGH)):
                for j in range(3):
                    last = nc.tensor.transpose(o[:, j * P:(j + 1) * P], wraw[:, 3 * k + j, :], ident[:])
                last.then_inc(wt_ps, 1)
            pe.wait_ge(wt_sb, 2)
            for l, o in enumerate((pGI, pAG, pF)):
                nc.tensor.matmul(o[:, 0:3 * P], wT[:, 3 + l, :], wT[:, 0:3, :].rearrange("p g e -> p (g e)"),
                                 start=True, stop=True).then_inc(wf_ps, 1)

            def step(q, s, exists):
                g, b = s % QUAD, s % 2
                if exists(s):
                    if layer(s) == 0:
                        hold(pe, h0hi_ok, made(q, "first", s))
                        hold(pe, h0lo_ok, made(q, "first", s))
                    else:
                        hold(pe, hthi_ok, made(q, "inner", s - 4))
                        hold(pe, htlo_ok, made(q, "inner", s - 4))
                    for k, (o, freed) in enumerate(((pR, r_ok), (pZ, z_ok), (pGH, rhn_ok))):
                        hold(pe, freed, made(q, "all", s - 1))
                        w = slice(k * P, (k + 1) * P)
                        last = three(o[:], whh_hi[:, w], whh_lo[:, w], hT_hi[:, g, :], hT_lo[:, g, :],
                                     start=True, stop=(k == 2))
                    last.then_inc(hh_ps, 1)
                u = s - 3
                if exists(u) and layer(u) == LAYERS - 1:
                    hold(pe, h_ok, made(q, "all", u))
                    if layer(u - 1) == LAYERS - 1:
                        hold(pe, x1_ok, made(q, "last", u - 1))
                    for j in range(GR):
                        last = nc.tensor.transpose(pF[:, j * P:(j + 1) * P], hT[:, u % QUAD, j * P:(j + 1) * P], ident[:])
                    last.then_inc(f_ps, 1)
                u = s + 1
                if exists(u):
                    if layer(u) == 0:
                        hold(pe, xn_ok, made(q, "first", u))
                        src = xn
                    else:
                        hold(pe, h_ok, made(q, "all", u - 4))
                        src = hT
                    for j in range(GR):
                        last = nc.tensor.transpose(pT[:, j * P:(j + 1) * P], src[:, u % QUAD, j * P:(j + 1) * P], ident[:])
                    last.then_inc(t_ps, 1)
                if exists(s):
                    hold(pe, aghi_ok, made(q, "all", s))
                    hold(pe, aglo_ok, made(q, "all", s))
                    for k, (o, done) in enumerate(((pR, r_ps), (pZ, z_ps), (pGI, in_ps))):
                        if k == 2:
                            hold(pe, cand_ok, made(q, "all", s - 1))
                        w = slice(k * P, (k + 1) * P)
                        three(o[:], wf_hi[:, layer(s), w], wf_lo[:, layer(s), w], ag_hi[:, b, :], ag_lo[:, b, :],
                              start=(k == 2), stop=True).then_inc(done, 1)
                if exists(u):
                    if s == -1:
                        pe.wait_ge(whi_done, LAYERS + 1)
                        pe.wait_ge(wlo_done, LAYERS + 1)
                    if layer(u) == 0:
                        hold(pe, adj_ok, made(q, "first", u))
                        hold(pe, x0hi_ok, made(q, "first", u))
                        hold(pe, x0lo_ok, made(q, "first", u))
                    else:
                        hold(pe, hnhi_ok, made(q, "later", u))
                        hold(pe, hnlo_ok, made(q, "later", u))
                    for j in range(GR):
                        c = slice(j * P, (j + 1) * P)
                        nc.tensor.matmul(pAG[:, c], hn_hi[:, u % 2, c], A[:, u % QUAD, c], start=True, stop=False)
                        last = nc.tensor.matmul(pAG[:, c], hn_lo[:, u % 2, c], A[:, u % QUAD, c], start=False, stop=True)
                    last.then_inc(ag_ps, 1)

            HB = (pR, pZ, pGH, pGI)

            def hidden(xb, chunks, done):
                for k in chunks:
                    w = slice(k * P, (k + 1) * P)
                    three(HB[k][:], w1_hi[:, w], w1_lo[:, w], hT_hi[:, xb, :], hT_lo[:, xb, :],
                          start=True, stop=True).then_inc(done, 1)

            def gate_step(s, c, t):
                if inside(s + 1, GROUPS):
                    b4 = (c + 1) % 4
                    pe.wait_ge(g_xn, s + 2)
                    hold(pe, g_xlo, s + 1)
                    for j in range(GR):
                        last = nc.tensor.transpose(pT[:, j * P:(j + 1) * P], xn[:, b4, j * P:(j + 1) * P], ident[:])
                    last.then_inc(g_t, 1)
                if inside(s, GROUPS):
                    if c == 0:
                        pe.wait_ge(w1_hi_done, 1)
                        pe.wait_ge(w1_lo_done, 1)
                        for read in (r_ok, z_ok, rhn_ok, cand_ok):
                            pe.wait_ge(read, QUADS * UNITS)
                    pe.wait_ge(g_xhi, s + 1)
                    pe.wait_ge(g_xlo, s + 1)
                    hold(pe, g_h, s * KC - 2)
                    hidden(c % 2, (0, 1), g_w1)
                if inside(s - 1, GROUPS):
                    if c == 1:
                        pe.wait_ge(ffn_in, FFN_LOADS)
                    pe.wait_ge(g_h, s * KC)
                    hold(pe, g_lgT, s - 1)
                    for k in range(KC):
                        last = nc.tensor.matmul(pAG[k * CT:(k + 1) * CT, :], wg_sb[:, k, :], HT[:, (c - 1) % 2, k, :],
                                                start=True, stop=True, tile_position=(0, k * CT))
                    last.then_inc(g_lg, 1)
                if inside(s, GROUPS):
                    hold(pe, g_h, s * KC)
                    hidden(c % 2, (2, 3), g_w1)
                if inside(s - 1, GROUPS):
                    if c == 1:
                        pe.wait_ge(c_dv, 2)
                    pe.wait_ge(g_lgT, s)
                    hold(pe, g_sh, s - 1)
                    for j in range(GR):
                        last = nc.tensor.matmul(pX[:, j * E:(j + 1) * E], lgT[:, j * P:(j + 1) * P], pick[:], start=True, stop=True)
                    last.then_inc(g_pick, 1)
                if inside(s - 2, GROUPS):
                    b = (c - 2) % 2
                    if c == 2:
                        pe.wait_ge(c_msk, 3)
                        pe.wait_ge(x1_ok, GROUPS)
                    pe.wait_ge(g_oh, s - 1)
                    hold(pe, g_pos, s - 2)
                    nc.tensor.matmul(pF[:, 0:(GR + 1) * E], before[:], oh[:, b, :, :].rearrange("p g e -> p (g e)"),
                                     start=True, stop=False)
                    for j in range(1, GR + 1):
                        last = nc.tensor.matmul(pF[:, j * E:(GR + 1) * E], ones[:],
                                                oh[:, b, 0:GR + 1 - j, :].rearrange("p g e -> p (g e)"),
                                                start=False, stop=(j == GR))
                    last.then_inc(g_rk, 1)

            gnn_steps(pe, step, gate_step)
            gate_steps(pe, gate_step)

            pe.wait_ge(tb, TABLE)
            for k in range(3):
                last = nc.tensor.matmul(pX[0:1, k * P:(k + 1) * P], tab[:, k:k + 1], ident[:], start=True, stop=True)
            last.then_inc(tab_ps, 1)
            pe.wait_ge(tab_ok, 1)

            def step(s, c, t):
                if inside(s, SGROUPS):
                    pe.wait_ge(e_xhi, s + 1)
                    pe.wait_ge(e_xlo, s + 1)
                    hold(pe, e_h, s * KC)
                    hidden(c % 2, range(KC), e_w1)
                if inside(s + 1, SGROUPS):
                    b4 = (c + 1) % 2
                    pe.wait_ge(e_xn, (s + 2) * GR)
                    for j in range(GR):
                        last = nc.tensor.transpose(pT[:, j * P:(j + 1) * P], xn[:, b4, j * P:(j + 1) * P], ident[:])
                    last.then_inc(e_t, 1)
                if inside(s - 1, SGROUPS):
                    b = (c - 1) % 2
                    o = (pAG, pF)[b]
                    pe.wait_ge(e_h, s * KC)
                    hold(pe, e_yb, (s - 2) * GR)
                    for j in range(GR):
                        at = pe.value_load(wd_tab[0:1, bass.ds((s - 1) * GR + j, 1)], min_val=0,
                                           max_val=(E - 1) * KC * P)
                        for k in range(KC):
                            last = nc.tensor.matmul(o[:, j * P:(j + 1) * P], HT[:, b, k, j * P:(j + 1) * P],
                                                    wd_sb[:, bass.ds(at + k * P, P)],
                                                    start=(k == 0), stop=(k == KC - 1))
                    last.then_inc(e_y, 1)

            expert_steps(pe, step)

        @block.scalar
        def _(act):
            act.dma_start(bi[:], b_ih.rearrange("(k p) -> p k", p=P), allow_slow_non_contiguous=True).then_inc(b_in, 16)
            act.dma_start(bh[:], b_hh.rearrange("(k p) -> p k", p=P), allow_slow_non_contiguous=True).then_inc(b_in, 16)
            act.wait_ge(wt_ps, 1)
            nc.scalar.activation(wT[:, 0:3, :].rearrange("p g e -> p (g e)"), pR[:, 0:3 * P], ACT.Copy).then_inc(wt_sb, 1)
            act.wait_ge(wt_ps, 3)
            nc.scalar.activation(wT[:, 3:6, :].rearrange("p g e -> p (g e)"), pGH[:, 0:3 * P], ACT.Copy).then_inc(wt_sb, 1)
            nc.scalar.activation(whh_hi[:], pZ[:, 0:3 * P], ACT.Copy).then_inc(whi_done, 1)
            for l, o in enumerate((pGI, pAG, pF)):
                act.wait_ge(wf_ps, l + 1)
                nc.scalar.activation(wf_hi[:, l, :], o[:, 0:3 * P], ACT.Copy).then_inc(whi_done, 1)
            act.wait_ge(c_dv, 1)

            def step(q, s, exists):
                b = s % 2
                if exists(s):
                    hold(act, ag_ps, made(q, "all", s))
                    nc.scalar.activation(ag_hi[:, b, :], pAG[:], ACT.Copy).then_inc(aghi_ok, 1)
                u = s - 1
                if exists(u):
                    hold(act, cand_ok, made(q, "all", u))
                    nc.scalar.activation(n_sb[:, u % 2, :], cand[:, u % 2, :], ACT.Tanh, bias=bi[:, 2:3]).then_inc(n_ok, 1)
                u = s + 1
                if exists(u) and layer(u) == 0:
                    hold(act, xn_ok, made(q, "first", u))
                    nc.scalar.activation(hn_hi[:, u % 2, :], xn[:, u % QUAD, :], ACT.Copy).then_inc(x0hi_ok, 1)
                u = s - 2
                if exists(u) and layer(u) < LAYERS - 1:
                    hold(act, h_ok, made(q, "all", u))
                    nc.scalar.activation(hT_hi[:, u % QUAD, :], hT[:, u % QUAD, :], ACT.Copy).then_inc(hthi_ok, 1)
                u = s + 1
                if exists(u):
                    hold(act, t_ps, made(q, "all", u))
                    if layer(u) == 0:
                        nc.scalar.activation(hT[:, u % QUAD, :], pT[:], ACT.Copy).then_inc(h0_ok, 1)
                        nc.scalar.activation(hT_hi[:, u % QUAD, :], pT[:], ACT.Copy).then_inc(h0hi_ok, 1)
                    else:
                        nc.scalar.activation(hn_hi[:, u % 2, :], pT[:], ACT.Copy).then_inc(hnhi_ok, 1)
                if exists(s):
                    hold(act, r_ps, made(q, "all", s))
                    nc.scalar.activation(r_sb[:, b, :], pR[:], ACT.Sigmoid, bias=bsum[:, 0:1]).then_inc(r_ok, 1)
                    hold(act, z_ps, made(q, "all", s))
                    nc.scalar.activation(z_sb[:, s % QUAD, :], pZ[:], ACT.Sigmoid, bias=bsum[:, 1:2]).then_inc(z_ok, 1)


            def gelus(hb, s, chunks, ready, done):
                for k in chunks:
                    hold(act, ready, s * KC + k + 1)
                    nc.scalar.activation(HT[:, hb, k, :], HB[k][:], ACT.Gelu, bias=b1c[:, k:k + 1]).then_inc(done, 1)

            HB = (pR, pZ, pGH, pGI)

            def gate_step(s, c, t):
                if c == -6:
                    act.wait_ge(ffn_in, FFN_LOADS)
                    nc.scalar.activation(w1_hi[:], w1raw[:], ACT.Copy).then_inc(w1_hi_done, 1)
                if inside(s + 1, GROUPS):
                    act.wait_ge(g_t, s + 2)
                    nc.scalar.activation(hT_hi[:, (c + 1) % 2, :], pT[:], ACT.Copy).then_inc(g_xhi, 1)
                if inside(s, GROUPS):
                    hold(act, g_lg, s - 1)
                    gelus(c % 2, s, (0, 1), g_w1, g_h)
                if inside(s - 1, GROUPS):
                    act.wait_ge(g_lg, s)
                    hold(act, g_pick, s - 1)
                    nc.scalar.activation(lgT[:], pAG[:], ACT.Identity, bias=bg_col[:, 0:1]).then_inc(g_lgT, 1)
                if inside(s - 2, GROUPS):
                    b = (c - 2) % 2
                    act.wait_ge(g_sh, s - 1)
                    hold(act, g_prob, s - 3)
                    nc.scalar.activation(th[:, b, :, :], sh[:, b, :, :], ACT.Tanh, scale=0.5).then_inc(g_th, 1)
                if inside(s, GROUPS):
                    gelus(c % 2, s, (2, 3), g_w1, g_h)
                if inside(s - 3, GROUPS):
                    b = (c - 3) % 2
                    act.wait_ge(g_tok, 1)
                    act.wait_ge(g_prob, s - 2)
                    hold(act, g_out[b], landed(t, 4, c - 5, 2))
                    nc.scalar.activation(stage[:, b, :, :], xrow[:, bass.ds((s - 3) * GR, GR), :], ACT.Copy).then_inc(g_rows, 1)

            gnn_steps(act, step, gate_step)
            gate_steps(act, gate_step)

            act.wait_ge(tab_ok, 1)
            halves = [(b, j) for b in range(2) for j in range(GR // 2, GR)]
            start = [act.value_load(row_tab[0:1, b * GR + j:b * GR + j + 1], min_val=0, max_val=E * REGION)
                     for b, j in halves]
            act.wait_ge(g_out[0], GROUPS // 2 * GR * 16)
            act.wait_ge(g_out[1], GROUPS // 2 * GR * 16)
            act.wait_ge(pad_ok, (E + 1) * 16)
            for n, (b, j) in enumerate(halves):
                act.dma_start(rows[:, b, j, :], sorted_rows[bass.ds(start[n], P), :]).then_inc(e_in[b], 16)

            def step(s, c, t):
                if inside(s, SGROUPS):
                    hold(act, e_y, s - 1)
                    gelus(c % 2, s, range(KC), e_w1, e_h)
                if inside(s + 1, SGROUPS):
                    act.wait_ge(e_t, s + 2)
                    nc.scalar.activation(hT_hi[:, (c + 1) % 2, :], pT[:], ACT.Copy).then_inc(e_xhi, 1)

            expert_steps(act, step)

        @block.vector
        def _(dve):
            tt, ts = nc.vector.tensor_tensor, nc.vector.tensor_scalar
            stt, red = nc.vector.scalar_tensor_tensor, nc.vector.tensor_reduce
            dve.wait_ge(c_gp, 8)

            def row_stats(b, graph, bn, bn_at, mv_done):
                for j in range(GR):
                    last = nc.vector.bn_stats(stats[:, b, j, :], xres[:, graph + j, :] if isinstance(graph, int)
                                              else xres[:, bass.ds(graph + j, 1), :].rearrange("p o c -> p (o c)"))
                last.then_inc(bn, 1)
                hold(dve, bn, bn_at)
                settle(dve)
                for j in range(GR):
                    last = nc.vector.bn_aggr(mv[:, b, j, :], stats[:, b, j, :])
                last.then_inc(mv_done, 1)

            def normalise(b, graph, done):
                for j in range(GR):
                    last = ts(xn[:, b, j * P:(j + 1) * P],
                              xres[:, graph + j, :] if isinstance(graph, int)
                              else xres[:, bass.ds(graph + j, 1), :].rearrange("p o c -> p (o c)"),
                              mv[:, b, j, 0:1], mv[:, b, j, 1:2],
                              ALU.subtract, ALU.mult)
                last.then_inc(done, 1)

            def weights_low():
                dve.wait_ge(whi_done, 1)
                tt(whh_lo[:], pZ[:, 0:3 * P], whh_hi[:].bitcast(fp32), ALU.subtract).then_inc(wlo_done, 1)
                dve.wait_ge(b_in, 32)
                tt(bsum[:], bi[:], bh[:], ALU.add).then_inc(c_dv, 1)
                for l, o in enumerate((pGI, pAG, pF)):
                    dve.wait_ge(whi_done, l + 2)
                    tt(wf_lo[:, l, :], o[:, 0:3 * P], wf_hi[:, l, :].bitcast(fp32), ALU.subtract).then_inc(wlo_done, 1)

            def step(q, s, exists):
                b = s % 2
                if exists(s):
                    hold(dve, aghi_ok, made(q, "all", s))
                    tt(ag_lo[:, b, :], pAG[:], ag_hi[:, b, :].bitcast(fp32), ALU.subtract).then_inc(aglo_ok, 1)
                u = s - 2
                if exists(u):
                    hold(dve, zd_ok, made(q, "all", u))
                    tt(hT[:, u % QUAD, :], n_sb[:, u % 2, :], diff[:, u % 2, :], ALU.add).then_inc(h_ok, 1)
                u = s + 1
                if exists(u):
                    if layer(u) == 0:
                        hold(dve, h0hi_ok, made(q, "first", u))
                        tt(hT_lo[:, u % QUAD, :], pT[:], hT_hi[:, u % QUAD, :].bitcast(fp32), ALU.subtract).then_inc(h0lo_ok, 1)
                    else:
                        hold(dve, hnhi_ok, made(q, "later", u))
                        tt(hn_lo[:, u % 2, :], pT[:], hn_hi[:, u % 2, :].bitcast(fp32), ALU.subtract).then_inc(hnlo_ok, 1)
                u = s - 3
                if exists(u) and layer(u) == LAYERS - 1:
                    hold(dve, f_ps, made(q, "last", u))
                    gx = xres[:, bass.ds(graph0(q, u), GR), :]
                    tt(gx, pF[:].rearrange("p (g n) -> p g n", g=GR), gx, ALU.add).then_inc(x1_ok, 1)
                if exists(s):
                    hold(dve, r_ok, made(q, "all", s))
                    stt(cand[:, b, :], pGH[:], bh[:, 2:3], r_sb[:, b, :], ALU.add, ALU.mult).then_inc(rhn_ok, 1)
                u = s + ahead(s)[1]
                if exists(u) and layer(u) == 0:
                    hold(dve, rstd_ok, made(q, "first", u))
                    normalise(u % QUAD, graph0(q, u), xn_ok)
                u = s + ahead(s)[0]
                if exists(u) and layer(u) == 0:
                    hold(dve, data_in, made(q, "first", u) * 32)
                    row_stats(u % QUAD, graph0(q, u), bn_ok, made(q, "first", u), mv_ok)
                u = s + 3
                if exists(u) and layer(u) == 0:
                    ts(A[:, u % QUAD, :].rearrange("p (g n) -> p g n", g=GR),
                       adj_i[:, bass.ds(graph0(q, u), GR), :], 0, None, ALU.not_equal).then_inc(adj_ok, 1)
                if exists(s):
                    hold(dve, in_ps, made(q, "all", s))
                    hold(dve, rhn_ok, made(q, "all", s))
                    tt(cand[:, b, :], pGI[:], cand[:, b, :], ALU.add).then_inc(cand_ok, 1)
                if isinstance(q, int) and s == -2:
                    weights_low()

            ROUNDS = 3
            NEWTON = 4 + 3 * ROUNDS - 1
            ROUTE, PLACE, SOFT = 3, 3, 4

            def gate_step(s, c, t):
                if c == -6:
                    dve.wait_ge(c_id, 2)
                    red(pick[:], ident[:].rearrange("p (k c) -> p c k", k=KC)[:, 0:E, :], AX.X, ALU.add).then_inc(c_dv, 1)
                    dve.wait_ge(w1_hi_done, 1)
                    tt(w1_lo[:], w1raw[:], w1_hi[:].bitcast(fp32), ALU.subtract).then_inc(w1_lo_done, 1)
                    nc.vector.tensor_copy(rev[:].rearrange("p g e -> p (g e)"), iot[:]).then_inc(tb, 1)
                    ts(tri[:], tri_i[:], 0.0, None, ALU.is_ge).then_inc(t_ch, 1)
                    nc.vector.tensor_copy(slot[:], slot_i[:]).then_inc(t_ch, 1)
                    nc.vector.tensor_copy(xrow[:, :, TOKEN], ids[:]).then_inc(g_tok, 1)
                    ts(ecap[:], ecap_i[:], float(REGION), None, ALU.mult).then_inc(tb, 1)
                    ts(base[:], ecap_i[:], float(REGION), None, ALU.mult).then_inc(tb, 1)
                    dve.wait_ge(x1_ok, (QUADS - 1) * QUAD)
                if c == 2:
                    dve.wait_ge(x1_ok, GROUPS)
                    dve.wait_ge(tb, 3)
                route, place = inside(s - 2, GROUPS), inside(s - 3, GROUPS)
                turn, norm, stat = inside(s + 1, GROUPS), inside(s + 2, GROUPS), inside(s + 6, GROUPS)
                b, d, b2, b6 = (c - 2) % 2, (c - 3) % 2, (c + 2) % 4, (c + 6) % 4
                n, m, k = (s - 2) * ROUTE, (s - 3) * PLACE, (s - 2) * SOFT
                lg = pX[:, 0:GR * E].rearrange("p (g e) -> p g e", g=GR)

                def rows_of(graph):
                    return xres[:, graph, :] if isinstance(graph, int) else \
                        xres[:, bass.ds(graph, 1), :].rearrange("p o c -> p (o c)")

                def kept(graph, start, end):
                    return xrow[:, graph, start:end] if isinstance(graph, int) else \
                        xrow[:, bass.ds(graph, 1), start:end].rearrange("p o c -> p (o c)")

                def normal(j):
                    return ts(xn[:, b2, j * P:(j + 1) * P], rows_of((s + 2) * GR + j),
                              kept((s + 2) * GR + j, MEAN, RSTD), kept((s + 2) * GR + j, RSTD, PROB), ALU.subtract, ALU.mult)

                def stat_of(j):
                    return nc.vector.bn_stats(stats[:, b6, j, :], rows_of((s + 6) * GR + j))

                if route:
                    dve.wait_ge(g_pick, s - 1)
                    red(mx[:, b, :], lg, AX.X, ALU.max).then_inc(g_dve, 1)
                if place:
                    dve.wait_ge(g_rk, s - 2)
                    tt(rk[:, d, :, :], pF[:, 0:GR * E].rearrange("p (g e) -> p g e", g=GR),
                       base[:].unsqueeze(1).to_broadcast([P, GR, E]), ALU.add).then_inc(g_place, 1)
                if stat:
                    stat_of(0)
                if route:
                    dve.wait_ge(g_dve, n + 1)
                    tt(sh[:, b, :, :], lg, mx[:, b, :].unsqueeze(2).to_broadcast([P, GR, E]),
                       ALU.subtract).then_inc(g_sh, 1)
                if place:
                    dve.wait_ge(g_place, m + 1)
                    tt(base[:], pF[:, GR * E:(GR + 1) * E], base[:], ALU.add).then_inc(g_base, 1)
                    tt(rk[:, d, :, :], rk[:, d, :, :], oh[:, d, 0:GR, :], ALU.mult).then_inc(g_place, 1)
                if stat:
                    stat_of(1)
                if route:
                    dve.wait_ge(g_sh, s - 1)
                    stt(mt[:, b, :, :], sh[:, b, :, :], 0.0, rev[:], ALU.is_ge, ALU.mult).then_inc(g_dve, 1)
                if place:
                    dve.wait_ge(g_place, m + 2)
                    red(posf[:, d, :], rk[:, d, :, :], AX.X, ALU.add).then_inc(g_place, 1)
                if stat:
                    stat_of(2)
                if route:
                    dve.wait_ge(g_dve, n + 2)
                    red(mv8[:, b, :], mt[:, b, :, :], AX.X, ALU.max).then_inc(g_dve, 1)
                if place:
                    dve.wait_ge(g_place, m + 3)
                    hold(dve, g_out[d], landed(t, 4, c - 5, 2))
                    nc.vector.tensor_copy(pos[:, d, :], posf[:, d, :]).then_inc(g_pos, 1)
                if stat:
                    stat_of(3).then_inc(g_bn, 1)
                if route:
                    dve.wait_ge(g_dve, n + 3)
                    tt(oh[:, b, 0:GR, :], mt[:, b, :, :], mv8[:, b, :].unsqueeze(2).to_broadcast([P, GR, E]),
                       ALU.is_equal).then_inc(g_oh, 1)
                if stat:
                    hold(dve, g_bn, s + 7)
                    settle(dve)
                    for j in range(GR):
                        last = nc.vector.bn_aggr(kept((s + 6) * GR + j, MEAN, PROB), stats[:, b6, j, :])
                    last.then_inc(g_mv, 1)
                if turn:
                    dve.wait_ge(g_xhi, s + 2)
                    tt(hT_lo[:, (c + 1) % 2, :], pT[:], hT_hi[:, (c + 1) % 2, :].bitcast(fp32), ALU.subtract).then_inc(g_xlo, 1)
                if norm:
                    dve.wait_ge(g_rstd, (s + 2) // 4 + 1 if isinstance(s, int) else t + (c + 2) // 4 + 1)
                    normal(0)
                if norm:
                    normal(1)
                if route:
                    dve.wait_ge(g_th, s - 1)
                    ts(den[:, b, :, :], th[:, b, :, :], -1.0, 1.0, ALU.mult, ALU.add).then_inc(g_pdve, 1)
                if norm:
                    normal(2)
                if route:
                    dve.wait_ge(g_pdve, k + 1)
                    nc.vector.reciprocal(num[:, b, :, :], den[:, b, :, :]).then_inc(g_pdve, 1)
                if norm:
                    normal(3).then_inc(g_xn, 1)
                if route:
                    dve.wait_ge(g_pdve, k + 2)
                    stt(ex[:, b, :, :], th[:, b, :, :], 1.0, num[:, b, :, :], ALU.add, ALU.mult).then_inc(g_pdve, 1)
                if route:
                    dve.wait_ge(g_pdve, k + 3)
                    red(ssum[:, b, :], ex[:, b, :, :], AX.X, ALU.add).then_inc(g_pdve, 1)
                if route:
                    dve.wait_ge(g_pdve, k + 4)
                    nc.vector.reciprocal(xrow[:, bass.ds((s - 2) * GR, GR), PROB], ssum[:, b, :]).then_inc(g_prob, 1)
                if stat and b6 == 3:
                    var = xrow[:, bass.ds((s + 3) * GR, 4 * GR), RSTD]
                    hold(dve, g_mv, s + 7)
                    q = ((s + 6) // 4 if isinstance(s, int) else t + (c + 6) // 4) * NEWTON
                    ts(nw_v[:], var, EPS, None, ALU.add).then_inc(g_nw, 1)
                    ts(nw_h[:], var, EPS, -0.5, ALU.add, ALU.mult).then_inc(g_nw, 1)
                    hold(dve, g_nw, q + 2)
                    ts(nw_i[:], nw_v[:].bitcast(i32), 1, None, ALU.arith_shift_right).then_inc(g_nw, 1)
                    hold(dve, g_nw, q + 3)
                    ts(nw_y[:].bitcast(i32), nw_i[:], -1.0, float(0x5f3759df), ALU.mult, ALU.add).then_inc(g_nw, 1)
                    for r in range(ROUNDS):
                        hold(dve, g_nw, q + 4 + 3 * r)
                        tt(nw_a[:], nw_y[:], nw_h[:], ALU.mult).then_inc(g_nw, 1)
                        hold(dve, g_nw, q + 5 + 3 * r)
                        tt(nw_a[:], nw_a[:], nw_y[:], ALU.mult).then_inc(g_nw, 1)
                        hold(dve, g_nw, q + 6 + 3 * r)
                        stt(nw_y[:] if r < ROUNDS - 1 else var, nw_a[:], 1.5, nw_y[:], ALU.add, ALU.mult).then_inc(
                            g_nw if r < ROUNDS - 1 else g_rstd, 1)
                if place:
                    dve.wait_ge(g_base, s - 2)

            gnn_steps(dve, step, gate_step)
            gate_steps(dve, gate_step)

            nc.vector.tensor_copy(pad_tab[:], base[0:1, :]).then_inc(tb, 1)
            tt(nf[:], base[:], ecap[:], ALU.subtract).then_inc(t_ch, 1)
            dve.wait_ge(t_ch, 3)
            ts(ni[:], nf[:], float(P - 1), None, ALU.add).then_inc(t_ch, 1)
            dve.wait_ge(t_ch, 4)
            ts(ni[:], ni[:], 7, None, ALU.arith_shift_right).then_inc(t_ch, 1)
            dve.wait_ge(t_ch, 5)
            nc.vector.tensor_copy(nblk[:], ni[:]).then_inc(t_ch, 1)
            dve.wait_ge(t_ch, 6)
            tt(cumt[:], tri[:], nblk[:].unsqueeze(1).to_broadcast([P, E, E]), ALU.mult).then_inc(t_ch, 1)
            ts(skip[:], nblk[:], float(-P), float(REGION), ALU.mult, ALU.add).then_inc(t_ch, 1)
            dve.wait_ge(t_ch, 8)
            red(cum[:], cumt[:], AX.X, ALU.add).then_inc(t_ch, 1)
            dve.wait_ge(t_ch, 9)
            ts(le[:], cum[:], slot[:, 0:1], None, ALU.is_le).then_inc(t_ch, 1)
            dve.wait_ge(t_ch, 10)
            red(esum[:], le[:], AX.X, ALU.add).then_inc(t_ch, 1)
            tt(cum[:], le[:], skip[:], ALU.mult).then_inc(t_ch, 1)
            dve.wait_ge(t_ch, 12)
            red(rsum[:], cum[:], AX.X, ALU.add).then_inc(t_ch, 1)
            ts(tab[:, 1:2], esum[:], float(E - 1), float(KC * P), ALU.min, ALU.mult).then_inc(tb, 1)
            ts(tab[:, 2:3], esum[:], float(E - 1), float(P), ALU.min, ALU.mult).then_inc(tb, 1)
            dve.wait_ge(t_ch, 13)
            stt(rsum[:], slot[:], float(P), rsum[:], ALU.mult, ALU.add).then_inc(t_ch, 1)
            dve.wait_ge(t_ch, 14)
            ts(tab[:, 0:1], rsum[:], float(E * REGION), None, ALU.min).then_inc(tb, 1)
            dve.wait_ge(tab_ps, 1)
            nc.vector.tensor_copy(tables[:], pX[0:1, 0:3 * P].rearrange("o (k p) -> o k p", k=3)).then_inc(tab_ok, 1)
            dve.wait_ge(tab_ok, 1)

            def step(s, c, t):
                if inside(s + 1, SGROUPS):
                    dve.wait_ge(e_xhi, s + 2)
                    tt(hT_lo[:, (c + 1) % 2, :], pT[:], hT_hi[:, (c + 1) % 2, :].bitcast(fp32), ALU.subtract).then_inc(e_xlo, 1)
                if inside(s + 2, SGROUPS):
                    b, r = (c + 2) % 2, (c + 2) % RING
                    dve.wait_ge(e_in[r], landed(t, RING, c + 2, RING))
                    hold(dve, e_t, s + 1)
                    for j in range(GR):
                        ts(xn[:, b, j * P:(j + 1) * P], rows[:, r, j, 0:P], rows[:, r, j, MEAN:MEAN + 1],
                           rows[:, r, j, RSTD:RSTD + 1], ALU.subtract, ALU.mult).then_inc(e_xn, 1)
                if inside(s - 1, SGROUPS):
                    b, r = (c - 1) % 2, (c - 1) % RING
                    o = (pAG, pF)[b]
                    hold(dve, e_out[b], landed(t, RING, c - 3, 2))
                    nc.vector.tensor_copy(home[:, b, :], rows[:, r, :, TOKEN]).then_inc(e_home, 1)
                    dve.wait_ge(e_y, s)

                    def product(j):
                        at = dve.value_load(bd_tab[0:1, bass.ds((s - 1) * GR + j, 1)], min_val=0, max_val=(E - 1) * P)
                        tt(yb[:, b, j, :], o[:, j * P:(j + 1) * P], bd_bc[:, bass.ds(at, P)], ALU.add).then_inc(e_yb, 1)

                    def result(j):
                        dve.wait_ge(e_yb, (s - 1) * GR + j + 1)
                        stt(yo[:, b, j, :], yb[:, b, j, :], rows[:, r, j, PROB:PROB + 1], rows[:, r, j, 0:P],
                            ALU.mult, ALU.add).then_inc(e_yo, 1)

                    product(0)
                    for j in range(1, GR):
                        product(j)
                        result(j - 1)
                    result(GR - 1)

            expert_steps(dve, step)


_INS = ['x', 'adj', 'L0_gnn_weight', 'L0_gnn_w_ih', 'L0_gnn_w_hh', 'L0_gnn_b_ih', 'L0_gnn_b_hh',
        'L0_ffn_W1', 'L0_ffn_b1', 'L0_ffn_Wg', 'L0_ffn_bg', 'L0_ffn_Wd', 'L0_ffn_bd']


def kernel(**inputs):
    import numpy as _np
    import concourse.bacc as _bacc
    from concourse import mybir as _mybir
    from concourse.bass_utils import run_bass_kernel_spmd as _run

    nc = _bacc.Bacc("TRN2", target_bir_lowering=False, num_devices=1)
    arrays, args = {}, []
    for name in _INS:
        a = _np.ascontiguousarray(inputs[name])
        arrays[f"in_{name}_dram"] = a
        args.append(nc.dram_tensor(f"in_{name}_dram", a.shape, _mybir.dt.from_np(a.dtype), kind="ExternalInput").ap())
    shape = inputs['x'].shape
    args.append(nc.dram_tensor("out_0_dram", shape, _mybir.dt.float32, kind="ExternalOutput").ap())
    build(nc, *args)
    r = _run(nc, [arrays], core_ids=[0])
    return r.results[0]["out_0_dram"]
```
